# Optimizing a Trainium2 kernel written in Bass

```python
import numpy as np
import jax
import jax.numpy as jnp

def _softmax(x, axis=-1):
    return jax.nn.softmax(x, axis=axis)

def _gelu(x):
    return jax.nn.gelu(x, approximate=True)

def _silu(x):
    return jax.nn.silu(x)

def _sigmoid(x):
    return jax.nn.sigmoid(x)

def _layernorm(x, axis=-1, eps=1e-05):
    m = jnp.mean(x, axis=axis, keepdims=True)
    v = jnp.var(x, axis=axis, keepdims=True)
    return (x - m) / jnp.sqrt(v + eps)

def _scatter_add(tgt, idx, src, axis=0):
    return tgt.at[idx].add(src)

def _segment_sum(src, seg, n):
    return jax.ops.segment_sum(src, seg, n)
kernel_name = 'mk_conv_seq_d4_conv_nchw512_r2_ae8121'

def setup_inputs(seed: int=0):
    np.random.seed(seed)
    _w = jnp.asarray

    def _rec_inputs():
        import jax
        import jax.numpy as jnp
        _gk = jax.random.key(seed)
        x = -0.0003929 + 0.9999 * jax.random.normal(jax.random.fold_in(_gk, 1), (8, 256, 32, 32), jnp.float32)
        return x
    x = _rec_inputs()

    def _L0_conv_setup():
        import jax, jax.numpy as jnp
        import numpy as np
        NUM_HEADS = 8
        NUM_GROUPS = 32
        EPS = 1e-05

        def group_norm(x, scale, bias):
            B, C, H, W = x.shape
            xr = x.reshape(B, NUM_GROUPS, C // NUM_GROUPS, H, W)
            mean = xr.mean(axis=(2, 3, 4), keepdims=True)
            var = xr.var(axis=(2, 3, 4), keepdims=True)
            xn = ((xr - mean) * jax.lax.rsqrt(var + EPS)).reshape(B, C, H, W)
            return xn * scale[None, :, None, None] + bias[None, :, None, None]
        key = jax.random.key(seed)
        ks = jax.random.split(key, 4)
        B, C, H, W = (8, 256, 32, 32)
        x = jax.random.normal(ks[0], (B, C, H, W), dtype=jnp.float32)
        gn_scale = jnp.ones((C,), dtype=jnp.float32)
        gn_bias = jnp.zeros((C,), dtype=jnp.float32)
        qkv_w = jax.random.normal(ks[1], (3 * C, C), dtype=jnp.float32) * C ** (-0.5)
        qkv_b = jnp.zeros((3 * C,), dtype=jnp.float32)
        proj_w = jax.random.normal(ks[2], (C, C), dtype=jnp.float32) * C ** (-0.5)
        proj_b = jnp.zeros((C,), dtype=jnp.float32)
        return {'x': x, 'gn_scale': gn_scale, 'gn_bias': gn_bias, 'qkv_w': qkv_w, 'qkv_b': qkv_b, 'proj_w': proj_w, 'proj_b': proj_b}
    _L0_conv_all = _L0_conv_setup()
    _L0_conv_in = {k: v for k, v in _L0_conv_all.items() if k in ('gn_scale', 'gn_bias', 'qkv_w', 'qkv_b', 'proj_w', 'proj_b')}
    del _L0_conv_all

    def _L1_conv_setup():
        import jax, jax.numpy as jnp
        import numpy as np
        H_CH = 32
        key = jax.random.key(seed)
        k0, k1, k2, k3 = jax.random.split(key, 4)
        inputs = jax.random.normal(k0, (8, 256, 32, 32), dtype=jnp.float32)
        Wa = jax.random.normal(k1, (192, 256), dtype=jnp.float32) * 0.05
        Wo = jax.random.normal(k2, (256, 128), dtype=jnp.float32) * 0.05
        gamma = jax.random.normal(k3, (1,), dtype=jnp.float32) * 0.1
        return {'inputs': inputs, 'Wa': Wa, 'Wo': Wo, 'gamma': gamma}
    _L1_conv_all = _L1_conv_setup()
    _L1_conv_in = {k: v for k, v in _L1_conv_all.items() if k in ('Wa', 'Wo', 'gamma')}
    del _L1_conv_all

    def _L2_conv_setup():
        import jax, jax.numpy as jnp
        import numpy as np
        GROUPS = 8
        NUM_HEADS = 8
        EPS = 1e-05

        def _group_norm(x, weight, bias):
            B, C, H, W = x.shape
            xg = x.reshape(B, GROUPS, C // GROUPS, H, W)
            mean = jnp.mean(xg, axis=(2, 3, 4), keepdims=True)
            var = jnp.var(xg, axis=(2, 3, 4), keepdims=True)
            xg = (xg - mean) * jax.lax.rsqrt(var + EPS)
            xn = xg.reshape(B, C, H, W)
            return xn * weight[None, :, None, None] + bias[None, :, None, None]
        key = jax.random.key(seed)
        ks = jax.random.split(key, 5)
        B, C, H, W = (8, 256, 32, 32)
        x = jax.random.normal(ks[0], (B, C, H, W), dtype=jnp.float32)
        gn_weight = jnp.ones((C,), dtype=jnp.float32)
        gn_bias = jnp.zeros((C,), dtype=jnp.float32)
        qkv_weight = jax.random.normal(ks[1], (3 * C, C), dtype=jnp.float32) * (1.0 / np.sqrt(C))
        qkv_bias = jax.random.normal(ks[2], (3 * C,), dtype=jnp.float32) * 0.02
        proj_weight = jax.random.normal(ks[3], (C, C), dtype=jnp.float32) * (1.0 / np.sqrt(C))
        proj_bias = jax.random.normal(ks[4], (C,), dtype=jnp.float32) * 0.02
        return {'x': x, 'gn_weight': gn_weight, 'gn_bias': gn_bias, 'qkv_weight': qkv_weight, 'qkv_bias': qkv_bias, 'proj_weight': proj_weight, 'proj_bias': proj_bias}
    _L2_conv_all = _L2_conv_setup()
    _L2_conv_in = {k: v for k, v in _L2_conv_all.items() if k in ('gn_weight', 'gn_bias', 'qkv_weight', 'qkv_bias', 'proj_weight', 'proj_bias')}
    del _L2_conv_all

    def _L3_conv_setup():
        import jax, jax.numpy as jnp
        import numpy as np
        GROUPS = 8
        HEADS = 8
        EPS = 1e-05

        def group_norm(x, gamma, beta):
            b, c, h, w = x.shape
            xg = x.reshape(b, GROUPS, c // GROUPS, h, w)
            mu = xg.mean(axis=(2, 3, 4), keepdims=True)
            var = xg.var(axis=(2, 3, 4), keepdims=True)
            xn = (xg - mu) / jnp.sqrt(var + EPS)
            xn = xn.reshape(b, c, h, w)
            return xn * gamma[None, :, None, None] + beta[None, :, None, None]
        key = jax.random.key(seed)
        ks = jax.random.split(key, 3)
        b, c, h, w = (8, 256, 32, 32)
        x = jax.random.normal(ks[0], (b, c, h, w), dtype=jnp.float32)
        gamma = jnp.ones((c,), dtype=jnp.float32)
        beta = jnp.zeros((c,), dtype=jnp.float32)
        w_qkv = jax.random.normal(ks[1], (3 * c, c), dtype=jnp.float32) * c ** (-0.5)
        w_out = jax.random.normal(ks[2], (c, c), dtype=jnp.float32) * c ** (-0.5)
        b_out = jnp.zeros((c,), dtype=jnp.float32)
        return {'x': x, 'gamma': gamma, 'beta': beta, 'w_qkv': w_qkv, 'w_out': w_out, 'b_out': b_out}
    _L3_conv_all = _L3_conv_setup()
    _L3_conv_in = {k: v for k, v in _L3_conv_all.items() if k in ('gamma', 'beta', 'w_qkv', 'w_out', 'b_out')}
    del _L3_conv_all
    return {'x': x, 'L0_conv_gn_scale': _L0_conv_in['gn_scale'], 'L0_conv_gn_bias': _L0_conv_in['gn_bias'], 'L0_conv_qkv_w': _L0_conv_in['qkv_w'], 'L0_conv_qkv_b': _L0_conv_in['qkv_b'], 'L0_conv_proj_w': _L0_conv_in['proj_w'], 'L0_conv_proj_b': _L0_conv_in['proj_b'], 'L1_conv_Wa': _L1_conv_in['Wa'], 'L1_conv_Wo': _L1_conv_in['Wo'], 'L1_conv_gamma': _L1_conv_in['gamma'], 'L2_conv_gn_weight': _L2_conv_in['gn_weight'], 'L2_conv_gn_bias': _L2_conv_in['gn_bias'], 'L2_conv_qkv_weight': _L2_conv_in['qkv_weight'], 'L2_conv_qkv_bias': _L2_conv_in['qkv_bias'], 'L2_conv_proj_weight': _L2_conv_in['proj_weight'], 'L2_conv_proj_bias': _L2_conv_in['proj_bias'], 'L3_conv_gamma': _L3_conv_in['gamma'], 'L3_conv_beta': _L3_conv_in['beta'], 'L3_conv_w_qkv': _L3_conv_in['w_qkv'], 'L3_conv_w_out': _L3_conv_in['w_out'], 'L3_conv_b_out': _L3_conv_in['b_out']}

def reference(x, L0_conv_gn_scale, L0_conv_gn_bias, L0_conv_qkv_w, L0_conv_qkv_b, L0_conv_proj_w, L0_conv_proj_b, L1_conv_Wa, L1_conv_Wo, L1_conv_gamma, L2_conv_gn_weight, L2_conv_gn_bias, L2_conv_qkv_weight, L2_conv_qkv_bias, L2_conv_proj_weight, L2_conv_proj_bias, L3_conv_gamma, L3_conv_beta, L3_conv_w_qkv, L3_conv_w_out, L3_conv_b_out):
    import jax
    import jax.numpy as jnp

    def _L0_conv_ref(x, gn_scale, gn_bias, qkv_w, qkv_b, proj_w, proj_b):
        import jax, jax.numpy as jnp
        import numpy as np
        NUM_HEADS = 8
        NUM_GROUPS = 32
        EPS = 1e-05

        def group_norm(x, scale, bias):
            B, C, H, W = x.shape
            xr = x.reshape(B, NUM_GROUPS, C // NUM_GROUPS, H, W)
            mean = xr.mean(axis=(2, 3, 4), keepdims=True)
            var = xr.var(axis=(2, 3, 4), keepdims=True)
            xn = ((xr - mean) * jax.lax.rsqrt(var + EPS)).reshape(B, C, H, W)
            return xn * scale[None, :, None, None] + bias[None, :, None, None]
        B, C, H, W = x.shape
        N = H * W
        dh = C // NUM_HEADS
        h = group_norm(x, gn_scale, gn_bias)
        qkv = jnp.einsum('bchw,oc->bohw', h, qkv_w) + qkv_b[None, :, None, None]
        qkv = qkv.reshape(B, 3, C, N)
        q = qkv[:, 0].reshape(B, NUM_HEADS, dh, N)
        k = qkv[:, 1].reshape(B, NUM_HEADS, dh, N)
        v = qkv[:, 2].reshape(B, NUM_HEADS, dh, N)
        attn = jnp.einsum('bhcn,bhdn->bhcd', q, k) * dh ** (-0.5)
        attn = jax.nn.softmax(attn, axis=-1)
        out = jnp.einsum('bhcd,bhdn->bhcn', attn, v).reshape(B, C, H, W)
        out = jnp.einsum('bchw,oc->bohw', out, proj_w) + proj_b[None, :, None, None]
        return x + out

    def _L1_conv_ref(inputs, Wa, Wo, gamma):
        import jax, jax.numpy as jnp
        import numpy as np
        H_CH = 32
        bs, c, height, width = inputs.shape
        hc = H_CH
        w = jnp.einsum('oi,bihw->bohw', Wa, inputs)
        query = w[:, :hc].reshape(bs, hc, height * width)
        key_ = w[:, hc:2 * hc].reshape(bs, hc, -1)
        value = w[:, 2 * hc:].reshape(bs, c // 2, -1)
        s = jnp.einsum('bcn,bcm->bnm', query, key_)
        attn = jax.nn.softmax(s, axis=2)
        y = jnp.einsum('bcm,bnm->bcn', value, attn)
        y = y.reshape(bs, c // 2, height, width)
        o = jnp.einsum('oi,bihw->bohw', Wo, y) * gamma[0] + inputs
        return o

    def _L2_conv_ref(x, gn_weight, gn_bias, qkv_weight, qkv_bias, proj_weight, proj_bias):
        import jax, jax.numpy as jnp
        import numpy as np
        GROUPS = 8
        NUM_HEADS = 8
        EPS = 1e-05

        def _group_norm(x, weight, bias):
            B, C, H, W = x.shape
            xg = x.reshape(B, GROUPS, C // GROUPS, H, W)
            mean = jnp.mean(xg, axis=(2, 3, 4), keepdims=True)
            var = jnp.var(xg, axis=(2, 3, 4), keepdims=True)
            xg = (xg - mean) * jax.lax.rsqrt(var + EPS)
            xn = xg.reshape(B, C, H, W)
            return xn * weight[None, :, None, None] + bias[None, :, None, None]
        B, C, H, W = x.shape
        hd = C // NUM_HEADS
        h = _group_norm(x, gn_weight, gn_bias)
        qkv = jnp.einsum('bchw,oc->bohw', h, qkv_weight) + qkv_bias[None, :, None, None]
        qkv = qkv.reshape(B, 3, NUM_HEADS, hd, H * W)
        q, k, v = (qkv[:, 0], qkv[:, 1], qkv[:, 2])
        attn = jnp.einsum('bncd,bncf->bndf', q, k) * hd ** (-0.5)
        attn = jax.nn.softmax(attn, axis=-1)
        out = jnp.einsum('bndf,bncf->bncd', attn, v)
        out = out.reshape(B, C, H, W)
        proj = jnp.einsum('bchw,oc->bohw', out, proj_weight) + proj_bias[None, :, None, None]
        return x + proj

    def _L3_conv_ref(x, gamma, beta, w_qkv, w_out, b_out):
        import jax, jax.numpy as jnp
        import numpy as np
        GROUPS = 8
        HEADS = 8
        EPS = 1e-05

        def group_norm(x, gamma, beta):
            b, c, h, w = x.shape
            xg = x.reshape(b, GROUPS, c // GROUPS, h, w)
            mu = xg.mean(axis=(2, 3, 4), keepdims=True)
            var = xg.var(axis=(2, 3, 4), keepdims=True)
            xn = (xg - mu) / jnp.sqrt(var + EPS)
            xn = xn.reshape(b, c, h, w)
            return xn * gamma[None, :, None, None] + beta[None, :, None, None]
        b, c, h, w = x.shape
        n = h * w
        dim_head = c // HEADS
        scale = dim_head ** (-0.5)
        xn = group_norm(x, gamma, beta)
        xf = xn.reshape(b, c, n)
        qkv = jnp.einsum('oc,bcn->bon', w_qkv, xf)
        q, k, v = jnp.split(qkv, 3, axis=1)
        q = q.reshape(b, HEADS, dim_head, n) * scale
        k = k.reshape(b, HEADS, dim_head, n)
        v = v.reshape(b, HEADS, dim_head, n)
        sim = jnp.einsum('bhdi,bhdj->bhij', q, k)
        attn = jax.nn.softmax(sim, axis=-1)
        out = jnp.einsum('bhij,bhdj->bhid', attn, v)
        out = out.transpose(0, 1, 3, 2).reshape(b, c, n)
        out = jnp.einsum('oc,bcn->bon', w_out, out) + b_out[None, :, None]
        return out.reshape(b, c, h, w) + xn

    def _gn(v, G=32, eps=1e-05):
        B_, C_, H_, W_ = v.shape
        g = v.reshape(B_, G, C_ // G, H_, W_)
        m = jnp.mean(g, axis=(2, 3, 4), keepdims=True)
        s = jnp.var(g, axis=(2, 3, 4), keepdims=True)
        return ((g - m) / jnp.sqrt(s + eps)).reshape(v.shape)

    def _ln_c(v, eps=1e-06):
        m = jnp.mean(v, axis=1, keepdims=True)
        s = jnp.var(v, axis=1, keepdims=True)
        return (v - m) / jnp.sqrt(s + eps)

    def _ln_t(v, eps=1e-05):
        m = jnp.mean(v, axis=-1, keepdims=True)
        s = jnp.var(v, axis=-1, keepdims=True)
        return (v - m) / jnp.sqrt(s + eps)

    def _to_tokens(v):
        B_, C_, H_, W_ = v.shape
        return v.reshape(B_, C_, H_ * W_).transpose(0, 2, 1)

    def _from_tokens(t, like):
        B_, C_, H_, W_ = like.shape
        return t.transpose(0, 2, 1).reshape(B_, C_, H_, W_)
    x = _L0_conv_ref(x, L0_conv_gn_scale, L0_conv_gn_bias, L0_conv_qkv_w, L0_conv_qkv_b, L0_conv_proj_w, L0_conv_proj_b)
    x = _L1_conv_ref(x, L1_conv_Wa, L1_conv_Wo, L1_conv_gamma)
    x = _L2_conv_ref(x, L2_conv_gn_weight, L2_conv_gn_bias, L2_conv_qkv_weight, L2_conv_qkv_bias, L2_conv_proj_weight, L2_conv_proj_bias)
    x = _L3_conv_ref(x, L3_conv_gamma, L3_conv_beta, L3_conv_w_qkv, L3_conv_w_out, L3_conv_b_out)
    return x

_drawn_inputs = setup_inputs


def setup_inputs(seed=0):
    import zlib

    import numpy as np

    out = dict(_drawn_inputs(seed))
    spreads = {'L0_conv_gn_scale': (1.0, 0.2),
     'L0_conv_gn_bias': (0.0, 0.1),
     'L0_conv_qkv_b': (0.0, 0.1),
     'L0_conv_proj_b': (0.0, 0.1),
     'L2_conv_gn_weight': (1.0, 0.2),
     'L2_conv_gn_bias': (0.0, 0.1),
     'L3_conv_gamma': (1.0, 0.2),
     'L3_conv_beta': (0.0, 0.1),
     'L3_conv_b_out': (0.0, 0.1)}
    factors = {'L2_conv_qkv_bias': 2.689, 'L2_conv_proj_bias': 2.932}
    for name, (base, spread) in spreads.items():
        noise = np.random.default_rng([zlib.crc32(name.encode()), seed]).standard_normal(out[name].shape)
        drawn = base * np.exp(spread * noise) if base else spread * noise
        out[name] = jnp.asarray(drawn.astype(out[name].dtype))
    for name, factor in factors.items():
        out[name] = (out[name] * factor).astype(out[name].dtype)
    return out
```

```python
from contextlib import ExitStack

import concourse.bass as bass
from concourse import mybir

F32 = mybir.dt.float32
F32R = mybir.dt.float32r
BF16 = mybir.dt.bfloat16
ALU = mybir.AluOpType
ACT = mybir.ActivationFunctionType
AX_X = mybir.AxisListType.X

P = 128
B = 8
C = 256
N = 1024
T = C // P
HEADS = 8
DH = C // HEADS
HPT = P // DH
QW = 512
NQ = N // QW
KC = N // P
QT = QW // P
HC1 = 32
VC1 = C // 2
EPS = 1e-5
SCALE = float(DH) ** -0.5
SPLIT = 3 * DH
MAXROW = SPLIT
ROWS = MAXROW + 2 * HPT
SCORE_BANKS = 3
MAX_BANKS = 2
PROB_SLOTS = 4
POOLED = 5
LAG = 2

COLS = {name: T * i for i, name in enumerate(
    ["gn0_scale", "gn0_bias", "bv0", "proj0_b", "gn2_scale", "gn2_bias", "bq2", "bk2", "bv2", "proj2_b",
     "gn3_scale", "gn3_bias", "proj3_b", "gamma1"])}
IDENT, MEAN8, MEAN32, ZERO = 0, P, 2 * P, 3 * P
CONST_COLS = 3 * P + T


class Count:

    def __init__(self, per_turn, more=0):
        self.per_turn, self.more = per_turn, more

    def __add__(self, n):
        return Count(self.per_turn, self.more + n)

    def __sub__(self, n):
        return Count(self.per_turn, self.more - n)

    def __mul__(self, n):
        return Count(self.per_turn * n, self.more * n)


class Turn:

    def __init__(self, eng, per_turns):
        self.eng = eng
        self.values = [eng.alloc_register(f"awaited{i}_{eng.engine.name}") for i in range(2)]
        self.base = {}
        for n in sorted(set(per_turns)):
            self.base[n] = eng.alloc_register(f"before_{eng.engine.name}_{n}")
            eng.reg_mov(self.base[n], n)
        self.used = set()

    def __mul__(self, n):
        return Count(n)

    def __add__(self, n):
        return Count(1, n)

    def at(self, count):
        self.used.add(count.per_turn)
        assert count.more >= 0
        if count.more == 0:
            return self.base[count.per_turn]
        self.values.reverse()
        self.eng.reg_add(self.values[0], self.base[count.per_turn], count.more)
        return self.values[0]

    def end(self):
        assert self.used == set(self.base), (self.used, set(self.base))
        for n, register in self.base.items():
            self.eng.reg_add(register, register, n)


class Events:

    def __init__(self, events):
        self.rank = {e: i + 1 for i, e in enumerate(events)}
        self.total = len(events)

    def event(self, rank):
        return [e for e, r in self.rank.items() if r == rank][0]

    def before(self, turn):
        return turn * self.total

    def after(self, turn, event):
        return turn * self.total + self.rank[event]


def attention_plan(layer, groups, steps, heads_a):
    def maxima(g):
        return [("max", layer, g, a) for a in range(heads_a)]

    plan = maxima(0) + [("maxrow", layer, 0)]
    late = []
    for g in range(groups):
        nxt = maxima(g + 1) if g + 1 < groups else []
        per = -(-len(nxt) // max(1, 4 * steps - 4))
        for s in range(steps):
            for j in range(4):
                plan.append(("score", layer, g, s, j))
                plan += nxt[:per]
                nxt = nxt[per:]
            late.append(("values", layer, g, s))
            if s == steps - 1:
                plan += nxt
                nxt = []
                if g + 1 < groups:
                    plan.append(("maxrow", layer, g + 1))
                late.append(("finish", layer, g))
            while len([x for x in late if x[0] == "values"]) > LAG:
                plan.append(late.pop(0))
                if late[0][0] == "finish":
                    plan.append(late.pop(0))
    return plan + late


def turn_plan():
    plan = [("load",)]
    plan += [("norm", 0)] + [("side", 0, "mean"), ("affine", 0), ("side", 0, "rows")]
    plan += [("side", 0, "turn", i) for i in range(4)]
    plan += [("side", 0, x) for x in ("gram", "keys", "logits")] + [("softmax0",)]
    plan += [("side", 0, x) for x in ("attv", "attb", "projb", "mix")]
    plan += [("side", 0, "out", i) for i in range(T * NQ)]
    plan += [("side", 1, "qk", i) for i in range(NQ)] + [("stack", 1)]
    plan += [("side", 1, "v", i) for i in range(2)]
    plan += attention_plan(1, NQ, 2, QT * NQ)
    plan += [("side", 1, "out", i) for i in range(T * NQ)]
    for layer in (2, 3):
        plan += [("norm", layer), ("side", layer, "mean"), ("affine", layer)]
        for m in range(4):
            plan += [("side", layer, "qk", m, i) for i in range(NQ)] + [("stack", layer, m)]
        plan += [("side", layer, "v", i) for i in range(4)]
        plan += attention_plan(layer, T * NQ, KC, HPT * QT * NQ)
        plan += [("side", layer, "out", i) for i in range(T * NQ)]
    return plan + [("store",)]


VECTOR_STEPS = 58


def build(nc, x, wqk0T, wv0, wp0T, rows0, waT1, woT1, wqkv2T, wp2T, wqkv3T, wp3T, cols, consts, out, steps_of=None):
    plan = turn_plan()
    side_events = []
    for e in plan:
        if e[0] in ("side", "maxrow"):
            side_events.append(e)
    SIDE = Events(side_events)
    MAXES = Events([e for e in plan if e[0] == "max"])
    SCORES = Events([e for e in plan if e[0] == "score"])
    VALUES = Events([e for e in plan if e[0] == "values"])
    GROUPS = Events([e for e in plan if e[0] == "finish"])
    MAXROWS = Events([e for e in plan if e[0] == "maxrow"])
    ADDS = Events([("add", e[1], e[2], a) for e in plan if e[0] == "finish"
                   for a in range(1, POOLED if e[1] != 1 else KC)])
    NORMS = Events([e for e in plan if e[0] == "norm"])
    LOWS = Events([e for e in plan if e[0] == "side" and e[2] == "qk"])
    STACKS = {s: Events([e for e in plan if e[0] == "stack" and e[1] != 1 and e[2] % 2 == s]) for s in range(2)}
    VSIDE = Events([e for e in plan if e[0] == "side" and e[2] == "v"])
    STACK_DMAS = 3 * HPT * 16
    STACK1_DMAS = 6 * 16

    ctx = ExitStack()
    with ctx:
        def sb(name, shape, dt=F32):
            return ctx.enter_context(nc.sbuf_tensor(name, shape, dt))

        def sem(name):
            return ctx.enter_context(nc.semaphore(name))

        wqk0_sb = sb("wqk0_sb", [P, T, 2 * C])
        wv0_sb = sb("wv0_sb", [P, T, C])
        wp_sb = {0: sb("wp0_sb", [P, T, C]), 2: sb("wp2_sb", [P, T, C]), 3: sb("wp3_sb", [P, T, C])}
        wa1_sb = sb("wa1_sb", [P, T, 2 * HC1 + VC1])
        wo1_sb = sb("wo1_sb", [P, C])
        wqkv_sb = {2: sb("wqkv2_sb", [P, T, 3 * C]), 3: sb("wqkv3_sb", [P, T, 3 * C])}
        rows0_sb = sb("rows0_sb", [1, 2 * C])
        cols_sb = sb("cols_sb", [P, len(COLS) * T])
        const_sb = sb("const_sb", [P, CONST_COLS])
        ident_bf = sb("ident_bf", [P, P], BF16)
        ones = sb("ones", [P, P])
        half_power = sb("half_power", [P, T])
        count_n = sb("count_n", [1, 1])
        projb2 = sb("projb2", [P, T])

        x_in = sb("x_in", [P, T, N])
        xs = sb("xs", [P, T, N])
        h = sb("h", [P, T, N])
        att = sb("att", [P, T, N])
        hT = sb("hT", [P, KC, C])
        vT = hT
        stats = sb("stats", [P, T, NQ, 6])
        mv = sb("mv", [P, T, 2])
        gm = sb("gm", [P, T, 2])
        gvar = sb("gvar", [P, T])
        rstd = sb("rstd", [P, T])
        ga = sb("ga", [P, T])
        gb = sb("gb", [P, T])
        small = sb("small", [P, T])
        hsum = sb("hsum", [P, T])
        su_rows = sb("su_rows", [1, 2 * C])
        gram = sb("gram", [P, T, C])
        gk = sb("gk", [P, T, C])
        l0 = sb("l0", [P, T, DH])
        l0T = sb("l0T", [P, T, DH])
        l0max = sb("l0max", [P, T])
        l0sum = sb("l0sum", [P, T])
        attb = sb("attb", [P, T])
        projb0 = sb("projb0", [P, T])
        attv = gram
        mixT = gk
        hi = [sb(f"hi{s}", [P, N], F32R) for s in range(2)]
        lo = [sb(f"lo{s}", [P, N], F32R) for s in range(2)]
        Q = sb("Q", [P, HEADS, N], F32R)
        K = sb("K", [P, HEADS, N], F32R)
        Q1, K1 = Q[:, 0, :], K[:, 0, :]
        maxpart = sb("maxpart", [P, QT * HPT, NQ])
        negmax = sb("negmax", [P, QT * HPT])
        maxsplit = sb("maxsplit", [P, QT * HPT, 2], BF16)
        prob = [sb(f"prob{i}", [P, 4, QW]) for i in range(PROB_SLOTS)]
        acc = [sb(f"acc{i}", [P, 4, QW]) for i in range(2)]
        rsum = gk[:, :, :].rearrange("p t c -> p (t c)")

        psum = ctx.enter_context(nc.psum_tensor("psum", [P, 8, QW], F32))
        score_bank = [psum[:, i, :] for i in range(SCORE_BANKS)]
        max_bank = [psum[:, SCORE_BANKS + i, :] for i in range(MAX_BANKS)]
        values_bank = psum[:, 5, :]
        sums_bank = psum[:, 6, :]
        side_bank = psum[:, 7, :]

        loaded = sem("loaded")
        kones = sem("kones")
        set_up = sem("set_up")
        biased = sem("biased")
        x_loaded = sem("x_loaded")
        x_taken = sem("x_taken")
        stored = sem("stored")
        result_ready = sem("result_ready")
        vstep = sem("vstep")
        moments_ready = sem("moments_ready")
        var_ready = sem("var_ready")
        rstd_ready = sem("rstd_ready")
        h_ready = sem("h_ready")
        side_full = sem("side_full")
        side_free = sem("side_free")
        hi_ready = sem("hi_ready")
        lo_ready = sem("lo_ready")
        stacked = [sem("stacked_q"), sem("stacked_k")]
        stacked1 = sem("stacked1")
        l0_ready = sem("l0_ready")
        l0_exp = sem("l0_exp")
        l0T_ready = sem("l0T_ready")
        max_full = sem("max_full")
        max_free = sem("max_free")
        maxsplit_ready = sem("maxsplit_ready")
        score_full = sem("score_full")
        exp_done = sem("exp_done")
        prob_used = sem("prob_used")
        added = sem("added")
        values_done = sem("values_done")
        group_done = sem("group_done")
        turned = sem("turned")
        block = ctx.enter_context(nc.Block())
        stack_dmas = STACKS[0].total * STACK_DMAS
        PER_TURN = {
            "sp": [1, LOWS.total, SCORES.total],
            "pool": [NORMS.total, SCORES.total, GROUPS.total, ADDS.total],
            "act": [1, SIDE.total, STACK1_DMAS, stack_dmas, VALUES.total, ADDS.total, SCORES.total],
            "dve": [1, 16, SIDE.total, NORMS.total, LOWS.total, MAXES.total, GROUPS.total, VECTOR_STEPS],
            "pe": [1, SIDE.total, NORMS.total, GROUPS.total, STACK1_DMAS, stack_dmas, MAXES.total, MAXROWS.total,
                   SCORES.total, ADDS.total],
        }

        STARTS = [
            (x_loaded, 16), (x_taken, 1), (stored, 16), (result_ready, 1), (vstep, VECTOR_STEPS),
            (moments_ready, NORMS.total), (var_ready, NORMS.total), (rstd_ready, NORMS.total), (h_ready, NORMS.total),
            (side_full, SIDE.total), (side_free, SIDE.total), (hi_ready, LOWS.total), (lo_ready, LOWS.total),
            (stacked[0], stack_dmas), (stacked[1], stack_dmas), (stacked1, STACK1_DMAS),
            (l0_ready, 1), (l0_exp, 1), (l0T_ready, 1), (max_full, MAXES.total), (max_free, MAXES.total),
            (maxsplit_ready, MAXROWS.total), (score_full, SCORES.total), (exp_done, SCORES.total),
            (prob_used, VALUES.total), (added, ADDS.total), (values_done, GROUPS.total), (group_done, GROUPS.total)]

        def col(name, t=None):
            a = COLS[name]
            return cols_sb[:, a:a + T] if t is None else cols_sb[:, a + t:a + t + 1]

        def image(ap, b):
            return ap[b].rearrange("(t p) n -> p t n", p=P)

        LOADS = [(wqk0_sb, wqk0T), (wv0_sb, wv0), (wp_sb[0], wp0T), (wa1_sb, waT1), (wqkv_sb[2], wqkv2T),
                 (wp_sb[2], wp2T), (wqkv_sb[3], wqkv3T), (wp_sb[3], wp3T)]
        N_LOADS = len(LOADS) + 4
        N_SETUP = 0

        def head_rows(j):
            return slice(DH * j, DH * (j + 1))

        @block.sync
        def _(sp):
            for semaphore, one_turn in STARTS:
                sp.sem_inc(semaphore, one_turn)
            for dst, src in LOADS:
                sp.dma_start(dst[:, :, :], src.rearrange("(t p) o -> p t o", p=P)).then_inc(loaded, 16)
            sp.dma_start(wo1_sb[:, :], woT1).then_inc(loaded, 16)
            sp.dma_start(rows0_sb[:, :], rows0).then_inc(loaded, 16)
            sp.dma_start(cols_sb[:, :], cols).then_inc(loaded, 16)
            sp.dma_start(const_sb[:, :], consts).then_inc(loaded, 16)
            b = Turn(sp, PER_TURN['sp'])
            with sp.Fori(0, B) as image_number:
                for e in plan:
                    if e[0] == "load":
                        sp.wait_ge(x_taken, b.at(b * 1))
                        sp.dma_start(x_in[:, :, :], image(x, image_number)).then_inc(x_loaded, 16)
                    elif e[0] == "stack" and e[1] == 1:
                        sp.wait_ge(lo_ready, b.at(LOWS.after(b, ("side", 1, "qk", NQ - 1))))
                        sp.wait_ge(score_full, b.at(SCORES.before(b)))
                        q, k = slice(0, HC1), slice(HC1, 2 * HC1)
                        for dst, src in ((Q1[0:32], hi[0][q]), (Q1[32:64], hi[0][q]), (Q1[64:96], lo[0][q]),
                                         (K1[0:32], hi[0][k]), (K1[32:64], lo[0][k]), (K1[64:96], hi[0][k])):
                            sp.dma_start(dst.bitcast(F32), src.bitcast(F32)).then_inc(stacked1, 16)
                    elif e[0] == "stack":
                        _, layer, m = e
                        t, s = m // 2, m % 2
                        low = b.at(LOWS.after(b, ("side", layer, "qk", m, NQ - 1)))
                        used = b.at(SCORES.before(b) if layer == 2
                                    else SCORES.after(b, ("score", 2, T * NQ - 1, KC - 1, 3)))
                        sp.wait_ge(score_full, used)
                        sp.wait_ge(lo_ready, low)
                        dst = (Q, K)[s]
                        parts = (hi[s], hi[s], lo[s]) if s == 0 else (hi[s], lo[s], hi[s])
                        for j in range(HPT):
                            for r, part in enumerate(parts):
                                sp.dma_start(dst[DH * r:DH * (r + 1), HPT * t + j, :].bitcast(F32),
                                             part[head_rows(j), :].bitcast(F32)).then_inc(stacked[s], 16)
                    elif e[0] == "store":
                        sp.wait_ge(result_ready, b.at(b + 1))
                        sp.dma_start(image(out, image_number), xs[:, :, :]).then_inc(stored, 16)
                b.end()
            sp.wait_ge(stored, 16 * (B + 1))

        @block.gpsimd
        def _(pool):
            pool.memset(K[MAXROW:ROWS, :, :].bitcast(F32), 0.0).then_inc(kones, 1)
            for j in range(HPT):
                for t in range(T):
                    pool.wait_ge(kones, 1 + 2 * (T * j + t))
                    pool.memset(K[MAXROW:MAXROW + 2 * j + 2, HPT * t + j, :].bitcast(F32), 1.0).then_inc(kones, 1)
                    pool.wait_ge(kones, 2 + 2 * (T * j + t))
                    pool.memset(K[MAXROW:MAXROW + max(2 * j, 1), HPT * t + j, :].bitcast(F32),
                                0.0 if j else 1.0).then_inc(kones, 1)
            pool.wait_ge(set_up, 4)
            b = Turn(pool, PER_TURN['pool'])
            with pool.Fori(0, B) as image_number:
                for e in plan:
                    if e[0] == "affine":
                        pool.wait_ge(var_ready, b.at(NORMS.after(b, ("norm", e[1]))))
                        pool.tensor_tensor(rstd[:, :], gvar[:, :], half_power[:, :], ALU.pow).then_inc(rstd_ready, 1)
                    elif e[0] == "finish":
                        _, layer, g = e
                        n = POOLED if layer != 1 else KC
                        for a in range(1, n):
                            add = ("add", layer, g, a)
                            if layer == 1:
                                step, j = a // 4, a % 4
                                total = acc[GROUPS.rank[e] % 2][:, 0, :]
                                first = prob[(VALUES.rank[("values", 1, g, 0)] - 1) % PROB_SLOTS][:, 0, :]
                                this = prob[(VALUES.rank[("values", 1, g, step)] - 1) % PROB_SLOTS][:, j, :]
                                pool.wait_ge(exp_done, b.at(SCORES.after(b, ("score", 1, g, step, j))))
                            else:
                                total = acc[GROUPS.rank[e] % 2][:, :, :]
                                first = prob[(VALUES.rank[("values", layer, g, 0)] - 1) % PROB_SLOTS][:, :, :]
                                this = prob[(VALUES.rank[("values", layer, g, a)] - 1) % PROB_SLOTS][:, :, :]
                                pool.wait_ge(exp_done, b.at(SCORES.after(b, ("score", layer, g, a, 3))))
                            if a == 1:
                                if GROUPS.rank[e] > 2:
                                    pool.wait_ge(values_done, b.at(GROUPS.after(b, e) - 2))
                                else:
                                    pool.wait_ge(values_done, b.at(GROUPS.before(b)))
                                prev = first
                            else:
                                pool.wait_ge(added, b.at(ADDS.after(b, add) - 1))
                                prev = total
                            pool.tensor_tensor(total, prev, this, ALU.add).then_inc(added, 1)
                b.end()

        @block.scalar
        def _(act):
            act.wait_ge(loaded, 16 * N_LOADS)
            act.activation(ident_bf[:, :], const_sb[:, IDENT:IDENT + P], ACT.Identity).then_inc(set_up, 1)
            b = Turn(act, PER_TURN['act'])
            with act.Fori(0, B) as image_number:
                for e in plan:
                    if e[0] == "side":
                        layer, what = e[1], e[2]
                        if layer == 0 and what in ("rows", "turn", "gram", "keys", "attv", "mix"):
                            act.wait_ge(side_full, b.at(SIDE.after(b, e)))
                            if what == "rows":
                                act.copy(su_rows[:, :], side_bank[0:1, :]).then_inc(side_free, 1)
                            elif what == "turn":
                                i = e[3]
                                act.copy(hT[:, 2 * i:2 * i + 2, :].rearrange("p a c -> p (a c)"),
                                         side_bank).then_inc(side_free, 1)
                            else:
                                dst = {"gram": gram, "keys": gk, "attv": attv, "mix": mixT}[what]
                                act.copy(dst[:, :, :].rearrange("p t c -> p (t c)"), side_bank).then_inc(side_free, 1)
                        elif what == "qk":
                            act.wait_ge(side_full, b.at(SIDE.after(b, e)))
                            if layer == 1:
                                i = e[3]
                                if i == 0:
                                    act.wait_ge(stacked[0], b.at(STACKS[0].before(b) * STACK_DMAS))
                                act.activation(hi[0][0:2 * HC1, i * QW:(i + 1) * QW], side_bank[0:2 * HC1, :],
                                               ACT.Identity).then_inc(hi_ready, 1)
                            else:
                                m, i = e[3], e[4]
                                t, s = m // 2, m % 2
                                if i == 0:
                                    if s == 0 and layer == 2 and t == 0:
                                        act.wait_ge(stacked1, b.at((b + 1) * STACK1_DMAS))
                                    act.wait_ge(stacked[s], b.at((STACKS[s].after(b, ("stack", layer, m)) - 1) * STACK_DMAS))
                                bias = col(("bq2", "bk2")[s], t) if layer == 2 else const_sb[:, ZERO:ZERO + 1]
                                act.activation(hi[s][:, i * QW:(i + 1) * QW], side_bank, ACT.Identity,
                                               bias=bias).then_inc(hi_ready, 1)
                        elif what == "v":
                            act.wait_ge(side_full, b.at(SIDE.after(b, e)))
                            i = e[3]
                            if layer == 1:
                                act.copy(vT[:, 4 * i:4 * i + 4, 0:VC1],
                                         side_bank.rearrange("p (a c) -> p a c", a=4)).then_inc(side_free, 1)
                            else:
                                act.copy(vT[:, 2 * i:2 * i + 2, :].rearrange("p a c -> p (a c)"),
                                         side_bank).then_inc(side_free, 1)
                    elif e[0] == "softmax0":
                        act.wait_ge(l0_ready, b.at(b + 1))
                        act.activation(l0[:, :, :], l0[:, :, :], ACT.Exp, scale=SCALE).then_inc(l0_exp, 1)
                    elif e[0] == "maxrow":
                        _, layer, g = e
                        act.wait_ge(side_full, b.at(SIDE.after(b, e)))
                        if layer == 1:
                            act.copy(Q1[MAXROW:MAXROW + 2, g * QW:(g + 1) * QW],
                                     side_bank[MAXROW:MAXROW + 2, :]).then_inc(side_free, 1)
                        else:
                            t, qc = g // NQ, g % NQ
                            src = side_bank[MAXROW:ROWS, :].unsqueeze(1).broadcast_to([2 * HPT, HPT, QW])
                            act.copy(Q[MAXROW:ROWS, HPT * t:HPT * (t + 1), qc * QW:(qc + 1) * QW],
                                     src).then_inc(side_free, 1)
                    elif e[0] == "score":
                        _, layer, g, s, j = e
                        r = VALUES.rank[("values", layer, g, s)]
                        if j == 0:
                            if r > PROB_SLOTS:
                                act.wait_ge(prob_used, b.at(VALUES.after(b, ("values", layer, g, s)) - PROB_SLOTS))
                                old = VALUES.event(r - PROB_SLOTS)
                            else:
                                act.wait_ge(prob_used, b.at(VALUES.before(b)))
                                old = None
                            if old is None:
                                act.wait_ge(added, b.at(ADDS.before(b)))
                            elif old[1] == 1:
                                act.wait_ge(added, b.at(ADDS.after(b, ("add", 1, old[2], (3, KC - 1)[old[3]]))))
                            elif old[3] < POOLED:
                                act.wait_ge(added, b.at(ADDS.after(b, ("add", old[1], old[2], max(1, old[3])))))
                        act.wait_ge(score_full, b.at(SCORES.after(b, e)))
                        act.activation(prob[(r - 1) % PROB_SLOTS][:, j, :],
                                       score_bank[(SCORES.rank[e] - 1) % SCORE_BANKS], ACT.Exp,
                                       scale=1.0 if layer == 1 else SCALE).then_inc(exp_done, 1)
                b.end()

        @block.vector
        def _(dve):
            dve.wait_ge(loaded, 16 * N_LOADS)
            dve.memset(ones[:, :], 1.0).then_inc(set_up, 1)
            dve.memset(half_power[:, :], -0.5).then_inc(set_up, 1)
            dve.memset(count_n[:, :], float(N)).then_inc(set_up, 1)
            dve.wait_ge(biased, 1)
            dve.tensor_tensor(projb2[:, :], side_bank[:, 0:T], col("proj2_b"), ALU.add).then_inc(biased, 1)

            b = Turn(dve, PER_TURN['dve'])
            with dve.Fori(0, B) as image_number:
                steps = [0]

                def own(ins):
                    steps[0] += 1
                    ins.then_inc(vstep, 1)
                    dve.wait_ge(vstep, b.at(b * VECTOR_STEPS + steps[0]))

                def norm_input(layer):
                    return x_in if layer == 0 else xs

                for e in plan:
                    if e[0] == "norm":
                        layer = e[1]
                        src = norm_input(layer)
                        if layer == 0:
                            dve.wait_ge(x_loaded, b.at((b + 1) * 16))
                        for t in range(T):
                            for i in range(NQ):
                                ins = dve.bn_stats(stats[:, t, i, :], src[:, t, i * QW:(i + 1) * QW])
                        own(ins)
                        dve.sem_inc(turned, 1)
                        for t in range(T):
                            ins = dve.bn_aggr(mv[:, t, :], stats[:, t, :, :].rearrange("p a s -> p (a s)"))
                        own(ins)
                        own(dve.tensor_tensor(small[:, :], mv[:, :, 0], mv[:, :, 0], ALU.mult))
                        dve.tensor_tensor(mv[:, :, 1], mv[:, :, 1], small[:, :], ALU.add).then_inc(moments_ready, 1)
                    elif e[0] == "affine":
                        layer = e[1]
                        src = norm_input(layer)
                        dve.wait_ge(rstd_ready, b.at(NORMS.after(b, ("norm", layer))))
                        own(dve.tensor_tensor(ga[:, :], rstd[:, :], col(f"gn{layer}_scale"), ALU.mult))
                        own(dve.tensor_tensor(small[:, :], gm[:, :, 0], ga[:, :], ALU.mult))
                        own(dve.tensor_tensor(gb[:, :], col(f"gn{layer}_bias"), small[:, :], ALU.subtract))
                        if layer == 0:
                            own(dve.tensor_tensor(small[:, :], mv[:, :, 0], ga[:, :], ALU.mult))
                            own(dve.tensor_tensor(small[:, :], small[:, :], gb[:, :], ALU.add))
                            own(dve.tensor_scalar(hsum[:, :], small[:, :], float(N), None, ALU.mult))
                        for t in range(T):
                            ins = dve.tensor_scalar(h[:, t, :], src[:, t, :], ga[:, t:t + 1], gb[:, t:t + 1],
                                                    ALU.mult, ALU.add)
                        ins.then_inc(h_ready, 1)
                    elif e[0] == "softmax0":
                        dve.wait_ge(side_full, b.at(SIDE.after(b, ("side", 0, "logits"))))
                        logits = side_bank[:, 0:T * DH].rearrange("p (t d) -> p t d", t=T)
                        own(dve.tensor_reduce(l0max[:, :], logits, AX_X, ALU.max))
                        dve.tensor_tensor(l0[:, :, :], logits, l0max[:, :].unsqueeze(2).broadcast_to([P, T, DH]),
                                          ALU.subtract).then_inc(l0_ready, 1)
                        dve.wait_ge(l0_ready, b.at(b + 1))
                        dve.sem_inc(side_free, 1)
                        dve.wait_ge(l0_exp, b.at(b + 1))
                        own(dve.tensor_reduce(l0sum[:, :], l0[:, :, :], AX_X, ALU.add))
                        own(dve.reciprocal(l0sum[:, :], l0sum[:, :]))
                        own(dve.tensor_tensor(l0[:, :, :], l0[:, :, :],
                                              l0sum[:, :].unsqueeze(2).broadcast_to([P, T, DH]), ALU.mult))
                        dve.transpose(l0T[:, :, :].rearrange("p t d -> p (t d)"),
                                      l0[:, :, :].rearrange("p t d -> p (t d)")).then_inc(l0T_ready, 1)
                    elif e[0] == "side":
                        layer, what = e[1], e[2]
                        if what == "mean":
                            dve.wait_ge(side_full, b.at(SIDE.after(b, e)))
                            dve.tensor_copy(gm[:, :, :].rearrange("p t s -> p (t s)"),
                                            side_bank[:, 0:2 * T]).then_inc(side_free, 1)
                            dve.wait_ge(side_free, b.at(SIDE.after(b, e)))
                            own(dve.tensor_tensor(small[:, :], gm[:, :, 0], gm[:, :, 0], ALU.mult))
                            dve.scalar_tensor_tensor(gvar[:, :], gm[:, :, 1], EPS, small[:, :], ALU.add,
                                                     ALU.subtract).then_inc(var_ready, 1)
                        elif what == "attb":
                            dve.wait_ge(side_full, b.at(SIDE.after(b, e)))
                            dve.tensor_copy(attb[:, :], side_bank[:, 0:T]).then_inc(side_free, 1)
                        elif what == "projb":
                            dve.wait_ge(side_full, b.at(SIDE.after(b, e)))
                            dve.tensor_tensor(projb0[:, :], side_bank[:, 0:T], col("proj0_b"),
                                              ALU.add).then_inc(side_free, 1)
                        elif what == "qk":
                            dve.wait_ge(hi_ready, b.at(LOWS.after(b, e)))
                            if layer == 1:
                                i = e[3]
                                part = slice(i * QW, (i + 1) * QW)
                                dve.tensor_tensor(lo[0][0:2 * HC1, part], side_bank[0:2 * HC1, :],
                                                  hi[0][0:2 * HC1, part].bitcast(F32), ALU.subtract).then_inc(lo_ready, 1)
                            else:
                                m, i = e[3], e[4]
                                t, s = m // 2, m % 2
                                part = slice(i * QW, (i + 1) * QW)
                                bias = col(("bq2", "bk2")[s], t) if layer == 2 else 0.0
                                dve.scalar_tensor_tensor(lo[s][:, part], side_bank, bias,
                                                         hi[s][:, part].bitcast(F32), ALU.add,
                                                         ALU.subtract).then_inc(lo_ready, 1)
                            dve.wait_ge(lo_ready, b.at(LOWS.after(b, e)))
                            dve.sem_inc(side_free, 1)
                        elif what == "out":
                            dve.wait_ge(side_full, b.at(SIDE.after(b, e)))
                            i = e[3]
                            t, part = i // NQ, slice((i % NQ) * QW, (i % NQ + 1) * QW)
                            if layer == 0:
                                if i == 0:
                                    dve.wait_ge(stored, b.at(b * 16))
                                ins = dve.scalar_tensor_tensor(xs[:, t, part], side_bank, projb0[:, t:t + 1],
                                                               x_in[:, t, part], ALU.add, ALU.add)
                            elif layer == 1:
                                ins = dve.scalar_tensor_tensor(xs[:, t, part], side_bank, col("gamma1", 0),
                                                               xs[:, t, part], ALU.mult, ALU.add)
                            elif layer == 2:
                                ins = dve.scalar_tensor_tensor(xs[:, t, part], side_bank, projb2[:, t:t + 1],
                                                               xs[:, t, part], ALU.add, ALU.add)
                            else:
                                ins = dve.scalar_tensor_tensor(xs[:, t, part], side_bank, col("proj3_b", t),
                                                               h[:, t, part], ALU.add, ALU.add)
                            ins.then_inc(side_free, 1)
                            dve.wait_ge(side_free, b.at(SIDE.after(b, e)))
                            if i == T * NQ - 1 and layer == 0:
                                dve.sem_inc(x_taken, 1)
                            elif i == T * NQ - 1 and layer == 3:
                                dve.sem_inc(result_ready, 1)
                    elif e[0] == "max":
                        _, layer, g, a = e
                        dve.wait_ge(max_full, b.at(MAXES.after(b, e)))
                        bank = max_bank[(MAXES.rank[e] - 1) % MAX_BANKS]
                        dve.tensor_reduce(maxpart[:, a // NQ, a % NQ:a % NQ + 1], bank, AX_X,
                                          ALU.max).then_inc(max_free, 1)
                    elif e[0] == "maxrow":
                        _, layer, g = e
                        n = QT if layer == 1 else QT * HPT
                        dve.wait_ge(max_free, b.at(MAXES.after(b, ("max", layer, g, n * NQ - 1))))
                        own(dve.tensor_reduce(negmax[:, 0:n], maxpart[:, 0:n, :], AX_X, ALU.max, negate=True))
                        if MAXROWS.rank[e] > 1:
                            dve.wait_ge(side_free, b.at(SIDE.after(b, MAXROWS.event(MAXROWS.rank[e] - 1))))
                        own(dve.tensor_copy(maxsplit[:, 0:n, 0], negmax[:, 0:n]))
                        dve.tensor_tensor(maxsplit[:, 0:n, 1], negmax[:, 0:n], maxsplit[:, 0:n, 0],
                                          ALU.subtract).then_inc(maxsplit_ready, 1)
                    elif e[0] == "finish":
                        _, layer, g = e
                        dve.wait_ge(values_done, b.at(GROUPS.after(b, e)))
                        own(dve.reciprocal(rsum[:, :], sums_bank))
                        t, qc = (0, g) if layer == 1 else (g // NQ, g % NQ)
                        dve.tensor_tensor(att[:, t, qc * QW:(qc + 1) * QW], values_bank, rsum[:, :],
                                          ALU.mult).then_inc(group_done, 1)
                assert steps[0] == VECTOR_STEPS
                if steps_of is not None:
                    steps_of.append(steps[0])
                b.end()

        @block.tensor
        def _(pe):
            pe.wait_ge(loaded, 16 * N_LOADS)
            pe.wait_ge(set_up, 4)
            pe.wait_ge(kones, 1 + 2 * HEADS)
            for ot in range(T):
                for t in range(T):
                    ins = pe.matmul(side_bank[:, ot:ot + 1], wp_sb[2][:, t, ot * P:(ot + 1) * P], col("bv2", t),
                                    start=(t == 0), stop=(t == T - 1))
            ins.then_inc(biased, 1)
            pe.wait_ge(biased, 2)

            b = Turn(pe, PER_TURN['pe'])
            with pe.Fori(0, B) as image_number:
                def side_start(e):
                    pe.wait_ge(side_free, b.at(SIDE.after(b, e) - 1))

                ident = const_sb[:, IDENT:IDENT + P]

                for e in plan:
                    if e[0] == "side":
                        layer, what = e[1], e[2]
                        side_start(e)
                        if what == "mean":
                            pe.wait_ge(moments_ready, b.at(NORMS.after(b, ("norm", layer))))
                            mean = MEAN8 if layer == 0 else MEAN32
                            ins = pe.matmul(side_bank[:, 0:2 * T], const_sb[:, mean:mean + P],
                                            mv[:, :, :].rearrange("p t s -> p (t s)"), start=True, stop=True)
                        elif what == "rows":
                            pe.wait_ge(h_ready, b.at(NORMS.after(b, ("norm", 0))))
                            for t in range(T):
                                pe.matmul(side_bank[0:1, t * P:(t + 1) * P], hsum[:, t:t + 1], ident,
                                          start=True, stop=True)
                            for t in range(T):
                                pe.matmul(side_bank[0:1, C:2 * C], hsum[:, t:t + 1], wqk0_sb[:, t, C:2 * C],
                                          start=(t == 0), stop=False)
                            ins = pe.matmul(side_bank[0:1, C:2 * C], count_n[:, :], rows0_sb[:, C:2 * C],
                                            start=False, stop=True)
                        elif what == "turn":
                            for a in range(2):
                                for t in range(T):
                                    kt = 2 * e[3] + a
                                    ins = pe.transpose(side_bank[:, a * C + t * P:a * C + (t + 1) * P],
                                                       h[:, t, kt * P:(kt + 1) * P], ident)
                        elif what == "gram":
                            for t in range(T):
                                for kt in range(KC):
                                    ins = pe.matmul(side_bank[:, t * C:(t + 1) * C], hT[:, kt, t * P:(t + 1) * P],
                                                    hT[:, kt, :], start=(kt == 0), stop=(kt == KC - 1))
                        elif what == "keys":
                            for it in range(T):
                                dst = side_bank[:, it * C:(it + 1) * C]
                                for t in range(T):
                                    pe.matmul(dst, gram[:, t, it * P:(it + 1) * P], wqk0_sb[:, t, C:2 * C],
                                              start=(t == 0), stop=False)
                                ins = pe.matmul(dst, su_rows[:, it * P:(it + 1) * P], rows0_sb[:, C:2 * C],
                                                start=False, stop=True)
                        elif what == "logits":
                            for t in range(T):
                                for j in range(HPT):
                                    ch = slice((HPT * t + j) * DH, (HPT * t + j + 1) * DH)
                                    dst = side_bank[head_rows(j), t * DH:(t + 1) * DH]
                                    for k in range(T):
                                        pe.matmul(dst, wqk0_sb[:, k, ch], gk[:, k, ch], start=(k == 0), stop=False,
                                                  tile_position=(0, DH * j))
                                    ins = pe.matmul(dst, rows0_sb[:, ch], su_rows[:, C + ch.start:C + ch.stop],
                                                    start=False, stop=True, tile_position=(0, DH * j))
                        elif what == "attv":
                            pe.wait_ge(l0T_ready, b.at(b + 1))
                            pe.sem_inc(turned, 1)
                            for t in range(T):
                                for j in range(HPT):
                                    r = head_rows(j)
                                    ins = pe.matmul(side_bank[r, t * C:(t + 1) * C], l0T[r, t, :], wv0_sb[r, t, :],
                                                    start=True, stop=True, tile_position=(DH * j, DH * j))
                        elif what == "attb":
                            pe.sem_inc(turned, 1)
                            for t in range(T):
                                for j in range(HPT):
                                    r = head_rows(j)
                                    ins = pe.matmul(side_bank[r, t:t + 1], l0T[r, t, :], col("bv0", t)[r, :],
                                                    start=True, stop=True, tile_position=(DH * j, DH * j))
                        elif what == "projb":
                            for ot in range(T):
                                for t in range(T):
                                    ins = pe.matmul(side_bank[:, ot:ot + 1], wp_sb[0][:, t, ot * P:(ot + 1) * P],
                                                    attb[:, t:t + 1], start=(t == 0), stop=(t == T - 1))
                        elif what == "mix":
                            for it in range(T):
                                for t in range(T):
                                    ins = pe.matmul(side_bank[:, it * C:(it + 1) * C],
                                                    attv[:, t, it * P:(it + 1) * P], wp_sb[0][:, t, :],
                                                    start=(t == 0), stop=(t == T - 1))
                        elif what == "qk":
                            if layer == 1:
                                part = slice(e[3] * QW, (e[3] + 1) * QW)
                                for t in range(T):
                                    ins = pe.matmul(side_bank[0:2 * HC1, :], wa1_sb[:, t, 0:2 * HC1], xs[:, t, part],
                                                    start=(t == 0), stop=(t == T - 1))
                            else:
                                m, i = e[3], e[4]
                                if m == 0 and i == 0:
                                    pe.wait_ge(h_ready, b.at(NORMS.after(b, ("norm", layer))))
                                o = (m % 2) * C + (m // 2) * P
                                for t in range(T):
                                    ins = pe.matmul(side_bank, wqkv_sb[layer][:, t, o:o + P],
                                                    h[:, t, i * QW:(i + 1) * QW], start=(t == 0), stop=(t == T - 1))
                        elif what == "v":
                            per, width = (4, VC1) if layer == 1 else (2, C)
                            src, w, o = (xs, wa1_sb, 2 * HC1) if layer == 1 else (h, wqkv_sb[layer], 2 * C)
                            for a in range(per):
                                kt = per * e[3] + a
                                for t in range(T):
                                    ins = pe.matmul(side_bank[:, a * width:(a + 1) * width],
                                                    src[:, t, kt * P:(kt + 1) * P], w[:, t, o:o + width],
                                                    start=(t == 0), stop=(t == T - 1))
                        elif what == "out":
                            i = e[3]
                            ot, part = i // NQ, slice((i % NQ) * QW, (i % NQ + 1) * QW)
                            if layer == 1:
                                if i == 0:
                                    pe.wait_ge(group_done, b.at(GROUPS.after(b, ("finish", 1, NQ - 1))))
                                ins = pe.matmul(side_bank, wo1_sb[:, ot * P:(ot + 1) * P], att[:, 0, part],
                                                start=True, stop=True)
                            else:
                                if layer == 0:
                                    w, src = mixT, h
                                else:
                                    w, src = wp_sb[layer], att
                                    if i == 0:
                                        pe.wait_ge(group_done, b.at(GROUPS.after(b, ("finish", layer, T * NQ - 1))))
                                for t in range(T):
                                    ins = pe.matmul(side_bank, w[:, t, ot * P:(ot + 1) * P], src[:, t, part],
                                                    start=(t == 0), stop=(t == T - 1))
                        ins.then_inc(side_full, 1)
                    elif e[0] == "max":
                        _, layer, g, a = e
                        r = MAXES.rank[e]
                        pe.wait_ge(max_free, b.at(MAXES.after(b, e) - MAX_BANKS if r > MAX_BANKS else MAXES.before(b)))
                        half = slice((a % NQ) * QW, (a % NQ + 1) * QW)
                        if layer == 1:
                            if g == 0 and a == 0:
                                pe.wait_ge(stacked1, b.at((b + 1) * STACK1_DMAS))
                            q = (g * QT + a // NQ) * P
                            left, right = Q1[0:SPLIT, q:q + P], K1[0:SPLIT, half]
                        else:
                            t, qc = g // NQ, g % NQ
                            if qc == 0 and a == 0:
                                for s in range(2):
                                    pair = ("stack", layer, 2 * t + s)
                                    pe.wait_ge(stacked[s], b.at(STACKS[s].after(b, pair) * STACK_DMAS))
                            qt, j = a // NQ // HPT, a // NQ % HPT
                            q = (qc * QT + qt) * P
                            left, right = Q[0:SPLIT, HPT * t + j, q:q + P], K[0:SPLIT, HPT * t + j, half]
                        pe.matmul(max_bank[(r - 1) % MAX_BANKS], left, right, start=True, stop=True).then_inc(max_full, 1)
                    elif e[0] == "maxrow":
                        _, layer, g = e
                        side_start(e)
                        pe.wait_ge(maxsplit_ready, b.at(MAXROWS.after(b, e)))
                        w = 1 if layer == 1 else HPT
                        for qt in range(QT):
                            ins = pe.matmul(side_bank[MAXROW:MAXROW + 2 * w, qt * P:(qt + 1) * P],
                                            maxsplit[:, qt * w:(qt + 1) * w, :].rearrange("p j s -> p (j s)"),
                                            ident_bf[:, :], start=True, stop=True, tile_position=(0, MAXROW))
                        ins.then_inc(side_full, 1)
                    elif e[0] == "score":
                        _, layer, g, s, j = e
                        r = SCORES.rank[e]
                        pe.wait_ge(exp_done, b.at(SCORES.after(b, e) - SCORE_BANKS if r > SCORE_BANKS else SCORES.before(b)))
                        if s == 0 and j == 0:
                            pe.wait_ge(side_free, b.at(SIDE.after(b, ("maxrow", layer, g))))
                        if layer == 1:
                            kt = 4 * s + j
                            left, right = K1[0:MAXROW + 2, kt * P:(kt + 1) * P], Q1[0:MAXROW + 2, g * QW:(g + 1) * QW]
                        else:
                            t, qc = g // NQ, g % NQ
                            left = K[0:ROWS, HPT * t + j, s * P:(s + 1) * P]
                            right = Q[0:ROWS, HPT * t + j, qc * QW:(qc + 1) * QW]
                        pe.matmul(score_bank[(r - 1) % SCORE_BANKS], left, right,
                                  start=True, stop=True).then_inc(score_full, 1)
                    elif e[0] == "values":
                        _, layer, g, s = e
                        slot = prob[(VALUES.rank[e] - 1) % PROB_SLOTS]
                        if s == 0:
                            pe.wait_ge(group_done, b.at(GROUPS.after(b, ("finish", layer, g)) - 1))
                        pe.wait_ge(exp_done, b.at(SCORES.after(b, ("score", layer, g, s, 3))))
                        if layer == 1:
                            for j in range(4):
                                kt = 4 * s + j
                                ins = pe.matmul(values_bank, vT[:, kt, 0:VC1], slot[:, j, :],
                                                start=(kt == 0), stop=(kt == KC - 1))
                        else:
                            for j in range(HPT):
                                head = HPT * (g // NQ) + j
                                ins = pe.matmul(values_bank[head_rows(j), :], vT[:, s, head * DH:(head + 1) * DH],
                                                slot[:, j, :], start=(s == 0), stop=(s == KC - 1),
                                                tile_position=(0, DH * j))
                            if s >= POOLED:
                                for j in range(HPT):
                                    ins = pe.matmul(sums_bank[head_rows(j), :], ones[:, 0:DH], slot[:, j, :],
                                                    start=(s == POOLED), stop=False, tile_position=(0, DH * j))
                        ins.then_inc(prob_used, 1)
                    elif e[0] == "finish":
                        _, layer, g = e
                        total = acc[GROUPS.rank[e] % 2]
                        if layer == 1:
                            pe.wait_ge(added, b.at(ADDS.after(b, ("add", 1, g, KC - 1))))
                            ins = pe.matmul(sums_bank, ones[:, :], total[:, 0, :], start=True, stop=True)
                        else:
                            pe.wait_ge(added, b.at(ADDS.after(b, ("add", layer, g, POOLED - 1))))
                            for j in range(HPT):
                                ins = pe.matmul(sums_bank[head_rows(j), :], ones[:, 0:DH], total[:, j, :],
                                                start=False, stop=True, tile_position=(0, DH * j))
                        ins.then_inc(values_done, 1)
                b.end()


def kernel(**inputs):
    import numpy as np
    import concourse.bacc as bacc
    from concourse.bass_utils import run_bass_kernel_spmd

    a = {k: np.asarray(v) for k, v in inputs.items()}

    def column(v):
        return v.reshape(T, P).T

    cols = [a["L0_conv_gn_scale"], a["L0_conv_gn_bias"], a["L0_conv_qkv_b"][2 * C:], a["L0_conv_proj_b"],
            a["L2_conv_gn_weight"], a["L2_conv_gn_bias"], a["L2_conv_qkv_bias"][:C], a["L2_conv_qkv_bias"][C:2 * C],
            a["L2_conv_qkv_bias"][2 * C:], a["L2_conv_proj_bias"], a["L3_conv_gamma"], a["L3_conv_beta"],
            a["L3_conv_b_out"], np.broadcast_to(a["L1_conv_gamma"], (C,))]
    consts = np.zeros((P, CONST_COLS), np.float32)
    for i in range(P):
        consts[i, IDENT + i] = 1.0
        for at, width in ((MEAN8, C // 32), (MEAN32, C // 8)):
            consts[i, at + i // width * width:at + (i // width + 1) * width] = 1.0 / width
    arrays = {
        "x": a["x"].reshape(B, C, N),
        "wqk0T": a["L0_conv_qkv_w"][:2 * C].T, "wv0": a["L0_conv_qkv_w"][2 * C:], "wp0T": a["L0_conv_proj_w"].T,
        "rows0": a["L0_conv_qkv_b"][:2 * C].reshape(1, 2 * C),
        "waT1": a["L1_conv_Wa"].T, "woT1": a["L1_conv_Wo"].T,
        "wqkv2T": a["L2_conv_qkv_weight"].T, "wp2T": a["L2_conv_proj_weight"].T,
        "wqkv3T": a["L3_conv_w_qkv"].T, "wp3T": a["L3_conv_w_out"].T,
        "cols": np.concatenate([column(v) for v in cols], axis=1), "consts": consts,
    }
    arrays = {k: np.ascontiguousarray(v) for k, v in arrays.items()}
    nc = bacc.Bacc("TRN2", target_bir_lowering=False, num_devices=1)
    args = {k: nc.dram_tensor(f"in_{k}", v.shape, F32, kind="ExternalInput").ap() for k, v in arrays.items()}
    out = nc.dram_tensor("out_0", (B, C, N), F32, kind="ExternalOutput").ap()
    build(nc, **args, out=out)
    r = run_bass_kernel_spmd(nc, [{f"in_{k}": v for k, v in arrays.items()}], core_ids=[0])
    return r.results[0]["out_0"].reshape(B, C, 32, 32)
```

```python
from contextlib import ExitStack

import concourse.bass as bass
from concourse import mybir

F32 = mybir.dt.float32
F32R = mybir.dt.float32r
BF16 = mybir.dt.bfloat16
ALU = mybir.AluOpType
ACT = mybir.ActivationFunctionType
AX_X = mybir.AxisListType.X

P = 128
B = 8
C = 256
N = 1024
T = C // P
HEADS = 8
DH = C // HEADS
HPT = P // DH
QW = 512
NQ = N // QW
KC = N // P
QT = QW // P
HC1 = 32
VC1 = C // 2
EPS = 1e-5
SCALE = float(DH) ** -0.5
SPLIT = 3 * DH
MAXROW = SPLIT
ROWS = MAXROW + 2 * HPT
SCORE_BANKS = 2
MAX_BANKS = 3
PROB_SLOTS = 4
POOLED = 7
AFTER_FINISH = 17
LAST_PIECE = 28
FIRST_MAX = 14
ROW_SLOTS = 3
LAG = 2 * HPT
STEPS = {1: KC // HPT, 2: KC, 3: KC}
MAXIMA = {1: QT * NQ, 2: HPT * QT * NQ, 3: HPT * QT * NQ}

COLS = {name: T * i for i, name in enumerate(
    ["gn0_scale", "gn0_bias", "bv0", "proj0_b", "gn2_scale", "gn2_bias", "bq2", "bk2", "bv2", "proj2_b",
     "gn3_scale", "gn3_bias", "proj3_b", "gamma1"])}
IDENT, MEAN8, MEAN32, ZERO = 0, P, 2 * P, 3 * P
CONST_COLS = 3 * P + T



def normalise(layer):
    return ([("stats", layer, t, i) for t in range(T) for i in range(NQ)]
            + [("norm", layer), ("side", layer, "mean"), ("power", layer), ("affine", layer)]
            + [("apply", layer, t) for t in range(T)])


def split_operand(layer, m):
    return [x for i in range(NQ) for x in (("side", layer, "qk", m, i), ("stack", layer, m, i))]


def side(layer, what, n):
    return [("side", layer, what, i) for i in range(n)]


def channel_attention(first):
    if first:
        return (normalise(0) + [("side", 0, "rows")] + side(0, "turn", KC // 2))
    return ([("side", 0, "gram"), ("side", 0, "keys"), [("side", 0, "logits"), ("softmax0",)]]
            + [("side", 0, x) for x in ("attv", "attb", "projb", "mix")] + side(0, "out", T * NQ))


def before_layer1():
    return split_operand(1, 0) + side(1, "v", 2)


def after_layer1(rest=True):
    more = split_operand(2, 0) + split_operand(2, 1) + side(2, "v", KC // 2)
    return side(1, "out", T * NQ) + [("save",)] + normalise(2) + (more if rest else [])


def spread(first, last, pieces):
    return [(first + (last - first) * (2 * i + 1) // (2 * len(pieces)), x) for i, x in enumerate(pieces)]


def group_sequence():
    after = AFTER_FINISH
    end = LAST_PIECE
    slots = KC * HPT
    late2_qk = split_operand(2, 2) + split_operand(2, 3)
    out3 = side(3, "out", T * NQ) + [("store",)]
    late2 = [(2, 0, spread(0, after, late2_qk[:4]) + spread(after, end, late2_qk[4:] + out3))]
    late2_first = [(2, 0, spread(0, end, late2_qk))]

    def layer2(prior, following):
        a = [(0, ("load",))] if following else []
        if prior:
            a += zip((1, 2, 3, 4, 5, 7, 8, 13, 14, 15), normalise(3))
        a.append((16, ("reload",)))
        if following:
            a += zip((8, 9, 10, 11, 12, 16, 17, 22, 23, 24), normalise(0))
        turned = ([("side", 0, "rows")] + side(0, "turn", KC // 2)) if following else []
        q3 = split_operand(3, 0) + split_operand(3, 1) if prior else []
        v3 = side(3, "v", KC // 2) if prior else []
        c = channel_attention(False) if following else []
        return [(2, 1, a), (2, 2, spread(0, end, turned + c[:3] + q3)), (2, 3, spread(0, end, c[3:] + v3))]

    out2 = side(2, "out", T * NQ)
    layer1 = [(1, 0, []), (1, 1, [])]
    q3 = split_operand(3, 2) + split_operand(3, 3)
    early3 = [x for x in q3[:4] if x[0] == "side"]
    out1 = after_layer1(False)

    def gap(pieces):
        return (None, None, pieces)

    first = ([gap([("load",)] + channel_attention(True) + channel_attention(False) + before_layer1())] + layer1
             + [gap(after_layer1())] + late2_first)
    second = layer2(False, True) + [gap(out2 + before_layer1())] + layer1 + [gap(after_layer1())] + late2_first
    steady = (layer2(True, True)
              + [(3, 0, spread(0, 12, before_layer1()) + spread(after, end, out2),
                  [(3, 1, 12, 0, 12), (1, 0, 8, 14, 21), (1, 0, None, 22, 22), (1, 1, 8, 23, 29)]),
                 (1, 0, [], [(1, 1, None, 2, 2), (3, 1, 10, 0, 7)]),
                 (1, 1, [(1, early3[0]), (4, early3[1])], [(3, 1, 10, 0, 4), (3, 1, None, 6, 6)]),
                 (3, 1, spread(0, 12, [x for x in q3 if x not in early3])
                  + [*zip((17, 18, 19, 20, 20, 21, 22, 23, 24, 25, 27, 28), out1)],
                  [(3, 2, 32, FIRST_MAX, slots - ROW_SLOTS - 2), (3, 2, None, slots - ROW_SLOTS, slots - ROW_SLOTS)]),
                 (3, 2, [*zip((3, 5, 6), out1[-3:])]
                  + spread(8, end, split_operand(2, 0) + split_operand(2, 1) + side(2, "v", KC // 2))),
                 (3, 3, [])] + late2)
    rest3 = [(3, 1, []), (3, 2, []), (3, 3, []), gap(out3)]
    last2 = layer2(True, False) + [(3, 0, spread(0, after, q3[:4]) + spread(after, end, out2 + q3[4:]))] + rest3
    last3 = ([gap(normalise(3) + split_operand(3, 0) + split_operand(3, 1) + side(3, "v", KC // 2)),
              (3, 0, spread(0, end, q3))] + rest3)
    return [first, second, steady, last2, last3]


RUNS = [1, 1, B - 2, 1, 1]
STEADY = 2


def flat(pieces):
    return [x for piece in pieces for x in (piece if isinstance(piece, list) else [piece])]


def plans():
    out = []
    late = []
    divides = []

    def advance(plan):
        x = late.pop(0)
        plan.append(x)
        if x[0] == "values" and x[3] == STEPS[x[1]] - 1:
            plan += [("finish",) + x[1:3], ("evacuate",) + x[1:3]]
            divides.extend(("divide",) + x[1:3] + (i,) for i in range(QT))

    turns = group_sequence()
    for n, groups in enumerate(turns):
        plan = []
        sought = {}

        def seek(layer, g, count):
            first = sought.get((layer, g), 0)
            sought[layer, g] = first + count
            return [("max", layer, g, a) for a in range(first, first + count)]

        for at, (layer, g, pieces, *maxima) in enumerate(groups):
            following = groups[at + 1] if at + 1 < len(groups) else turns[n + 1][0] if n + 1 < len(turns) else (None,)
            if layer is None:
                while late:
                    advance(plan)
                plan += divides + flat(pieces)
                divides.clear()
                if following[0] is not None and at + 1 < len(groups):
                    plan += seek(*following[:2], MAXIMA[following[0]])
                    plan += [("maxrow",) + following[:2], ("rowcopy",) + following[:2]]
                continue
            slots = STEPS[layer] * HPT
            if maxima:
                maxima = maxima[0]
            elif following[0] is not None:
                maxima = [following[:2] + (MAXIMA[following[0]], 0, slots - ROW_SLOTS - 2),
                          following[:2] + (None, slots - ROW_SLOTS, slots - ROW_SLOTS)]
            pieces = sorted(pieces, key=lambda x: x[0])
            for slot in range(slots):
                s, j = slot // HPT, slot % HPT
                plan.append(("score", layer, g, s, j))
                late.append(("values", layer, g, s) if j == HPT - 1 else ("value", layer, g, s, j))
                for to_layer, to_g, count, low, high in maxima:
                    if count is None:
                        rowcopy_at = low if to_layer == 1 else low + 1
                        plan += [(x, to_layer, to_g) for x, y in (("maxrow", low), ("rowcopy", rowcopy_at)) if slot == y]
                    elif low <= slot <= high:
                        due = [count * (x - low) // (high - low + 1) for x in (slot, slot + 1)]
                        plan += seek(to_layer, to_g, due[1] - due[0])
                if divides and slot % 2 == 0:
                    plan.append(divides.pop(0))
                rows = [x[0] for x in plan if x[0] in ("maxrow", "rowcopy")]
                while pieces and (pieces[0][0] <= slot or slot == slots - 1) and rows[-1:] != ["maxrow"]:
                    plan += flat([pieces.pop(0)[1]])
                while len(late) > LAG:
                    advance(plan)
        for i, x in enumerate(plan):
            assert x[0] != "maxrow" or "side" not in [y[0] for y in plan[i:plan.index(("rowcopy",) + x[1:])]]
        out.append(plan)
    assert not late and not divides
    return out


class Events:

    def __init__(self, all_plans, events_of, weight=lambda e: 1):
        self.rank, self.events, self.weight = [], [], weight
        for plan in all_plans:
            events = [x for e in plan for x in events_of(e)]
            self.events.append(events)
            rank, n = {}, 0
            for e in events:
                n += weight(e)
                rank[e] = n
            self.rank.append(rank)
        self.total = [sum(weight(e) for e in events) for events in self.events]
        self.start = [sum(self.total[j] * RUNS[j] for j in range(i)) for i in range(len(all_plans))]
        self.ahead = 0 if self.start[STEADY] else 1

    def number(self, turn, e):
        return self.start[turn.n] + self.events[turn.n].index(e)

    def events_before(self, turn, here):
        return sum(turn.place[e] < turn.place[here] for e in self.events[turn.n])

    def slot(self, turn, e):
        assert self.total[STEADY] % PROB_SLOTS == 0
        return self.number(turn, e) % PROB_SLOTS


class Turn:

    def __init__(self, eng, all_plans, n, used=()):
        self.eng, self.n, self.plan = eng, n, all_plans[n]
        self.place = {}
        for i, e in enumerate(self.plan):
            self.place[e] = i
        self.base, self.used = {}, set()
        if n == STEADY:
            name = eng.engine.name
            self.values = [eng.alloc_register(f"awaited{i}_{name}") for i in range(2)]
            for i, events in enumerate(used):
                self.base[events] = eng.alloc_register(f"before{i}_{name}")
                eng.reg_mov(self.base[events], events.start[n] + events.ahead)

    def value(self, events, more):
        if self.n != STEADY:
            return events.start[self.n] + events.ahead + more
        self.used.add(events)
        assert events in self.base, events.events[self.n][:3]
        if more == 0:
            return self.base[events]
        self.values.reverse()
        self.eng.reg_add(self.values[0], self.base[events], more)
        return self.values[0]

    def before(self, events):
        return self.value(events, 0)

    def after(self, events, e, less=0):
        return self.value(events, events.rank[self.n][e] - less)

    def until(self, events, here):
        n = sum(events.weight(e) for e in events.events[self.n] if self.place[e] < self.place[here])
        return self.value(events, n)

    def last(self, events, any_of, here, at=None):
        ranks = [events.rank[self.n][e] for e in any_of
                 if e in events.rank[self.n] and self.place[at or e] < self.place[here]]
        if ranks:
            return self.value(events, max(ranks))
        prior = [self.n - 1] + ([self.n] if self.n == STEADY else [])
        back = [events.total[i] - events.rank[i][e] for i in prior for e in any_of
                if i >= 0 and e in events.rank[i]]
        return self.value(events, -min(back)) if back else None

    def steps_back(self, starts, start, n):
        i = starts.events[self.n].index(start) - n
        if i >= 0:
            return starts.events[self.n][i]
        prior = [self.n - 1] + ([self.n] if self.n == STEADY else [])
        found = {starts.events[k][i] for k in prior if k >= 0}
        assert len(found) <= 1
        return found.pop() if found else None

    def end(self):
        assert self.used == set(self.base), [x.events[self.n][:2] for x in set(self.base) - self.used]
        for events, register in self.base.items():
            self.eng.reg_add(register, register, events.total[self.n])


def build(nc, x, wqk0T, wv0, wp0T, rows0, waT1, woT1, wqkv2T, wp2T, wqkv3T, wp3T, cols, consts, scratch, out):
    PLANS = plans()

    def when(test, weight=lambda e: 1):
        return Events(PLANS, lambda e: [e] if test(e) else [], weight)

    LOADS_X = when(lambda e: e[0] == "load", lambda e: 16)
    SAVES = when(lambda e: e[0] == "save", lambda e: 16)
    RELOADS = when(lambda e: e[0] == "reload", lambda e: 16)
    STORES = when(lambda e: e[0] == "store", lambda e: 16)
    SIDE = when(lambda e: e[0] in ("side", "maxrow"))
    MAXES = when(lambda e: e[0] == "max")
    SCORES = when(lambda e: e[0] == "score")
    VALUES = when(lambda e: e[0] == "values")
    GROUPS = when(lambda e: e[0] == "finish")
    MAXROWS = when(lambda e: e[0] == "maxrow")
    NORMS = when(lambda e: e[0] == "norm")
    SOFTMAX0 = when(lambda e: e[0] == "softmax0")
    PIECES = when(lambda e: e[0] == "side" and e[2] == "qk")

    STEP_STARTS = when(lambda e: e[0] == "score" and e[4] == 0)

    def adds(e):
        if e[0] != "values":
            return []
        _, layer, g, s = e
        tiles = range(HPT * s, HPT * (s + 1)) if layer == 1 else [s]
        return [("add", layer, g, a) for a in tiles if a and (layer == 1 or a < POOLED)]

    ADDS = Events(PLANS, adds)
    STACKED = [Events(PLANS, lambda e, s=s: [e] if e[0] == "stack" and e[-1] % 2 == s else [],
                      lambda e: 16 * (6 if e[1] == 1 else 3)) for s in range(2)]
    OWN = {"stats": 1, "norm": 2, "softmax0": 4, "maxrow": 2, "divide": 1}

    def own_steps(e):
        if e[0] == "affine":
            return 6 if e[1] == 0 else 3
        if e[0] == "side":
            return 1 if e[2] == "mean" else 0
        return OWN.get(e[0], 0)

    VSTEPS = when(own_steps, own_steps)

    ctx = ExitStack()
    with ctx:
        def sb(name, shape, dt=F32):
            return ctx.enter_context(nc.sbuf_tensor(name, shape, dt))

        def sem(name):
            return ctx.enter_context(nc.semaphore(name))

        wqk0_sb = sb("wqk0_sb", [P, T, 2 * C])
        wv0_sb = sb("wv0_sb", [P, T, C])
        wp_sb = {0: sb("wp0_sb", [P, T, C]), 2: sb("wp2_sb", [P, T, C]), 3: sb("wp3_sb", [P, T, C])}
        wa1_sb = sb("wa1_sb", [P, T, 2 * HC1 + VC1])
        wo1_sb = sb("wo1_sb", [P, C])
        wqkv_sb = {2: sb("wqkv2_sb", [P, T, 3 * C]), 3: sb("wqkv3_sb", [P, T, 3 * C])}
        rows0_sb = sb("rows0_sb", [1, 2 * C])
        cols_sb = sb("cols_sb", [P, len(COLS) * T])
        const_sb = sb("const_sb", [P, CONST_COLS])
        ident_bf = sb("ident_bf", [P, P], BF16)
        ones = sb("ones", [P, P])
        half_power = sb("half_power", [P, T])
        count_n = sb("count_n", [1, 1])
        projb2 = sb("projb2", [P, T])

        xa = sb("xa", [P, T, N])
        xb = sb("xb", [P, T, N])
        ha = sb("ha", [P, T, N])
        hb = sb("hb", [P, T, N])
        images = {0: xa, 2: xa, 3: xb}
        normed = {0: ha, 2: ha, 3: hb}
        att = sb("att", [P, T, N])
        att1 = att[:, 1, :]
        vT2 = sb("vT2", [P, KC, C])
        vT3 = sb("vT3", [P, KC, C])
        hT = vT3
        stats = sb("stats", [P, T, NQ, 6])
        mv = sb("mv", [P, T, 2])
        gm = sb("gm", [P, T, 2])
        gvar = sb("gvar", [P, T])
        rstd = sb("rstd", [P, T])
        ga = sb("ga", [P, T])
        gb = sb("gb", [P, T])
        small = sb("small", [P, T])
        hsum = sb("hsum", [P, T])
        su_rows = att[0:1, 1, 0:2 * C]
        products0 = sb("products0", [P, 2, T, C])
        gram, gk = products0[:, 0], products0[:, 1]
        vT1 = products0[:, :, :, :].rearrange("p a t c -> p (a t c)").rearrange("p (k c) -> p k c", c=VC1)
        vT = {1: vT1, 2: vT2, 3: vT3}
        attv, mixT = gram, gk
        l0 = sb("l0", [P, T, DH])
        l0T = sb("l0T", [P, T, DH])
        l0max = sb("l0max", [P, T])
        l0sum = sb("l0sum", [P, T])
        attb = sb("attb", [P, T])
        projb0 = sb("projb0", [P, T])
        hi = [sb(f"hi{s}", [P, QW], F32R) for s in range(2)]
        lo = [sb(f"lo{s}", [P, QW], F32R) for s in range(2)]
        Q = sb("Q", [P, HEADS, N], F32R)
        K = sb("K", [P, HEADS, N], F32R)
        Q1, K1 = Q[:, HPT, :], K[:, HPT, :]
        maxpart = {layer: sb(f"maxpart{layer}", [P, QT * HPT, NQ]) for layer in (1, 2)}
        maxpart[3] = maxpart[2]
        negmax = sb("negmax", [P, QT * HPT])
        maxsplit = sb("maxsplit", [P, QT * HPT, 2], BF16)
        prob = [sb(f"prob{i}", [P, HPT, QW]) for i in range(PROB_SLOTS)]
        acc = sb("acc", [P, HPT, QW])
        rsum = sb("rsum", [P, QW])

        psum = ctx.enter_context(nc.psum_tensor("psum", [P, 8, QW], F32))
        score_bank = [psum[:, i, :] for i in range(SCORE_BANKS)]
        max_bank = [psum[:, SCORE_BANKS + i, :] for i in range(MAX_BANKS)]
        values_bank = psum[:, 5, :]
        sums_bank = psum[:, 6, :]
        side_bank = psum[:, 7, :]

        loaded = sem("loaded")
        kones = sem("kones")
        set_up = sem("set_up")
        biased = sem("biased")
        x_loaded = sem("x_loaded")
        saved = sem("saved")
        reloaded = sem("reloaded")
        stored = sem("stored")
        vstep = sem("vstep")
        moments_ready = sem("moments_ready")
        var_ready = sem("var_ready")
        rstd_ready = sem("rstd_ready")
        affine_ready = sem("affine_ready")
        h_ready = sem("h_ready")
        side_full = sem("side_full")
        side_free = sem("side_free")
        hi_ready = sem("hi_ready")
        lo_ready = sem("lo_ready")
        stacked = [sem("stacked0"), sem("stacked1")]
        l0_ready = sem("l0_ready")
        l0_exp = sem("l0_exp")
        l0T_ready = sem("l0T_ready")
        max_full = sem("max_full")
        max_free = sem("max_free")
        maxsplit_ready = sem("maxsplit_ready")
        score_full = sem("score_full")
        exp_done = sem("exp_done")
        prob_used = sem("prob_used")
        added = sem("added")
        values_done = sem("values_done")
        evacuated = sem("evacuated")
        group_done = sem("group_done")
        turned = sem("turned")
        block = ctx.enter_context(nc.Block())

        SEMAPHORES = [
            (x_loaded, LOADS_X), (saved, SAVES), (reloaded, RELOADS), (stored, STORES), (vstep, VSTEPS),
            (moments_ready, NORMS), (var_ready, NORMS), (rstd_ready, NORMS), (affine_ready, NORMS), (h_ready, NORMS),
            (side_full, SIDE), (side_free, SIDE), (hi_ready, PIECES), (lo_ready, PIECES),
            (stacked[0], STACKED[0]), (stacked[1], STACKED[1]), (l0_ready, SOFTMAX0), (l0_exp, SOFTMAX0),
            (l0T_ready, SOFTMAX0), (max_full, MAXES), (max_free, MAXES), (maxsplit_ready, MAXROWS),
            (score_full, SCORES), (exp_done, SCORES), (prob_used, VALUES), (added, ADDS), (values_done, GROUPS),
            (evacuated, GROUPS), (group_done, GROUPS)]

        def col(name, t=None):
            a = COLS[name]
            return cols_sb[:, a:a + T] if t is None else cols_sb[:, a + t:a + t + 1]

        def image(ap, b):
            return ap[b].rearrange("(t p) n -> p t n", p=P)

        LOADS = [(wqk0_sb, wqk0T), (wv0_sb, wv0), (wp_sb[0], wp0T), (wa1_sb, waT1), (wqkv_sb[2], wqkv2T),
                 (wp_sb[2], wp2T), (wqkv_sb[3], wqkv3T), (wp_sb[3], wp3T)]
        N_LOADS = len(LOADS) + 4

        def head_rows(j):
            return slice(DH * j, DH * (j + 1))

        def run(eng, program, used):
            for n in range(len(PLANS)):
                b = Turn(eng, PLANS, n, used)
                if n == STEADY:
                    with eng.Fori(n - 1, n - 1 + RUNS[n]) as number:
                        program(b, number)
                        b.end()
                else:
                    program(b, sum(RUNS[:n]) - 1)

        @block.sync
        def _(sp):
            for semaphore, events in SEMAPHORES:
                if events.ahead:
                    sp.sem_inc(semaphore, events.ahead)
            for dst, src in LOADS:
                sp.dma_start(dst[:, :, :], src.rearrange("(t p) o -> p t o", p=P)).then_inc(loaded, 16)
            sp.dma_start(wo1_sb[:, :], woT1).then_inc(loaded, 16)
            sp.dma_start(rows0_sb[:, :], rows0).then_inc(loaded, 16)
            sp.dma_start(cols_sb[:, :], cols).then_inc(loaded, 16)
            sp.dma_start(const_sb[:, :], consts).then_inc(loaded, 16)

            def program(b, number):
                for e in b.plan:
                    if e[0] == "load":
                        done = b.last(NORMS, [("norm", 2)], e)
                        if done is not None:
                            sp.wait_ge(h_ready, done)
                        sp.dma_start(xa[:, :, :], image(x, number + 1)).then_inc(x_loaded, 16)
                    elif e[0] == "save":
                        sp.wait_ge(side_free, b.after(SIDE, ("side", 1, "out", T * NQ - 1)))
                        sp.dma_start(image(scratch, number + 1), xa[:, :, :]).then_inc(saved, 16)
                    elif e[0] == "reload":
                        done = b.last(NORMS, [("norm", 3)], e)
                        if done is not None:
                            sp.wait_ge(h_ready, done)
                        sp.wait_ge(saved, b.last(SAVES, [("save",)], e))
                        sp.dma_start(xb[:, :, :], image(scratch, number)).then_inc(reloaded, 16)
                    elif e[0] == "stack":
                        _, layer, m, i = e
                        t, s, part = m // 2, m % 2, slice(i * QW, (i + 1) * QW)
                        low = b.after(PIECES, ("side", layer, "qk", m, i))
                        users = [(2, T * NQ - 1)] if layer == 1 else [(user, NQ * t + NQ - 1) for user in (2, 3)]
                        if layer != 1 and t == T - 1:
                            users.append((1, NQ - 1))
                        used = b.last(SCORES, [("score", user, g, STEPS[user] - 1, 3) for user, g in users], e)
                        if used is not None:
                            sp.wait_ge(score_full, used)
                        sp.wait_ge(lo_ready, low)
                        if layer == 1:
                            q, k = slice(0, HC1), slice(HC1, 2 * HC1)
                            for dst, r, src in ((Q1, 0, hi[i][q]), (Q1, 1, hi[i][q]), (Q1, 2, lo[i][q]),
                                                (K1, 0, hi[i][k]), (K1, 1, lo[i][k]), (K1, 2, hi[i][k])):
                                sp.dma_start(dst[DH * r:DH * (r + 1), part].bitcast(F32),
                                             src.bitcast(F32)).then_inc(stacked[i], 16)
                        else:
                            dst = (Q, K)[s]
                            for r, src in enumerate((hi[i], hi[i], lo[i]) if s == 0 else (hi[i], lo[i], hi[i])):
                                sp.dma_start(dst[DH * r:DH * (r + 1), HPT * t:HPT * (t + 1), part].bitcast(F32),
                                             src[:, :].bitcast(F32)).then_inc(stacked[i], 16)
                    elif e[0] == "store":
                        sp.wait_ge(side_free, b.after(SIDE, ("side", 3, "out", T * NQ - 1)))
                        sp.dma_start(image(out, number - 1), hb[:, :, :]).then_inc(stored, 16)

            run(sp, program, [NORMS, SIDE, SCORES, PIECES, SAVES])
            sp.wait_ge(stored, STORES.ahead + 16 * B)

        @block.gpsimd
        def _(pool):
            pool.memset(K[MAXROW:ROWS, :, :].bitcast(F32), 0.0).then_inc(kones, 1)
            for j in range(HPT):
                for t in range(T):
                    pool.wait_ge(kones, 1 + 2 * (T * j + t))
                    pool.memset(K[MAXROW:MAXROW + 2 * j + 2, HPT * t + j, :].bitcast(F32), 1.0).then_inc(kones, 1)
                    pool.wait_ge(kones, 2 + 2 * (T * j + t))
                    pool.memset(K[MAXROW:MAXROW + max(2 * j, 1), HPT * t + j, :].bitcast(F32),
                                0.0 if j else 1.0).then_inc(kones, 1)
            pool.wait_ge(set_up, 4)

            def program(b, number):
                for e in b.plan:
                    if e[0] == "power":
                        pool.wait_ge(var_ready, b.after(NORMS, ("norm", e[1])))
                        pool.tensor_tensor(rstd[:, :], gvar[:, :], half_power[:, :], ALU.pow).then_inc(rstd_ready, 1)
                    elif e[0] == "values":
                        _, layer, g, s = e
                        slot, before = prob[VALUES.slot(b, e)], prob[VALUES.slot(b, e) - 1]
                        for add in adds(e):
                            a = add[3]
                            j = a % HPT if layer == 1 else HPT - 1
                            pool.wait_ge(exp_done, b.last(SCORES, [("score", layer, g, s, j)], e))
                            if layer == 1:
                                total, this, first = acc[:, 0, :], slot[:, j, :], slot[:, 0, :]
                            else:
                                total, this, first = acc[:, :, :], slot[:, :, :], before[:, :, :]
                            if a == 1:
                                pool.wait_ge(values_done, b.until(GROUPS, e))
                            else:
                                pool.wait_ge(added, b.after(ADDS, add, 1))
                            pool.tensor_tensor(total, first if a == 1 else total, this, ALU.add).then_inc(added, 1)

            run(pool, program, [NORMS, SCORES, GROUPS, ADDS])

        @block.scalar
        def _(act):
            act.wait_ge(loaded, 16 * N_LOADS)
            act.activation(ident_bf[:, :], const_sb[:, IDENT:IDENT + P], ACT.Identity).then_inc(set_up, 1)

            def program(b, number):
                for e in b.plan:
                    if e[0] == "apply":
                        _, layer, t = e
                        if layer == 0 and t == 0:
                            read = b.last(SIDE, [("side", 2, "v", KC // 2 - 1)], e)
                            if read is not None:
                                act.wait_ge(side_free, read)
                        elif layer == 3 and t == 0:
                            left = b.last(STORES, [("store",)], e)
                            if left is not None:
                                act.wait_ge(stored, left)
                        if t == 0:
                            act.wait_ge(affine_ready, b.after(NORMS, ("norm", layer)))
                        ins = act.activation(normed[layer][:, t, :], images[layer][:, t, :], ACT.Identity,
                                             bias=gb[:, t:t + 1], scale=ga[:, t:t + 1])
                        if t == T - 1:
                            ins.then_inc(h_ready, 1)
                    elif e[0] == "side":
                        layer, what = e[1], e[2]
                        if layer == 0 and what in ("rows", "turn", "gram", "keys", "attv", "mix"):
                            act.wait_ge(side_full, b.after(SIDE, e))
                            if what == "rows":
                                act.copy(su_rows[:, :], side_bank[0:1, :]).then_inc(side_free, 1)
                            elif what == "turn":
                                i = e[3]
                                act.copy(hT[:, 2 * i:2 * i + 2, :].rearrange("p a c -> p (a c)"),
                                         side_bank).then_inc(side_free, 1)
                            else:
                                dst = {"gram": gram, "keys": gk, "attv": attv, "mix": mixT}[what]
                                act.copy(dst[:, :, :].rearrange("p t c -> p (t c)"), side_bank).then_inc(side_free, 1)
                        elif what == "qk":
                            m, i = e[3], e[4]
                            act.wait_ge(stacked[i], b.until(STACKED[i], e))
                            act.wait_ge(side_full, b.after(SIDE, e))
                            if layer == 1:
                                act.activation(hi[i][0:2 * HC1, :], side_bank[0:2 * HC1, :],
                                               ACT.Identity).then_inc(hi_ready, 1)
                            else:
                                bias = col(("bq2", "bk2")[m % 2], m // 2) if layer == 2 else const_sb[:, ZERO:ZERO + 1]
                                act.activation(hi[i][:, :], side_bank, ACT.Identity, bias=bias).then_inc(hi_ready, 1)
                        elif what == "v":
                            act.wait_ge(side_full, b.after(SIDE, e))
                            i, per = e[3], KC // 2 if layer == 1 else 2
                            act.copy(vT[layer][:, per * i:per * (i + 1), :],
                                     side_bank.rearrange("p (a c) -> p a c", a=per)).then_inc(side_free, 1)
                    elif e[0] == "softmax0":
                        act.wait_ge(l0_ready, b.after(SOFTMAX0, e))
                        act.activation(l0[:, :, :], l0[:, :, :], ACT.Exp, scale=SCALE).then_inc(l0_exp, 1)
                    elif e[0] in ("maxrow", "rowcopy"):
                        _, layer, g = e
                        if e[0] == "maxrow":
                            act.wait_ge(side_full, b.after(SIDE, e))
                        if layer == 1:
                            if e[0] == "rowcopy":
                                act.copy(Q1[MAXROW:MAXROW + 2, g * QW:(g + 1) * QW],
                                         side_bank[MAXROW:MAXROW + 2, :]).then_inc(side_free, 1)
                        else:
                            t, qc, half = g // NQ, g % NQ, HPT // 2
                            head = HPT * t + (half if e[0] == "rowcopy" else 0)
                            ins = act.copy(Q[MAXROW:ROWS, head:head + half, qc * QW:(qc + 1) * QW],
                                           side_bank[MAXROW:ROWS, :].unsqueeze(1).broadcast_to([2 * HPT, half, QW]))
                            if e[0] == "rowcopy":
                                ins.then_inc(side_free, 1)
                    elif e[0] == "evacuate":
                        _, layer, g = e
                        act.wait_ge(values_done, b.after(GROUPS, ("finish", layer, g)))
                        dst = att1 if layer == 1 else att[:, g // NQ, :]
                        act.copy(dst[:, (g % NQ) * QW:(g % NQ + 1) * QW], values_bank).then_inc(evacuated, 1)
                    elif e[0] == "score":
                        _, layer, g, s, j = e
                        start = ("score", layer, g, s, 0)
                        if j == 0:
                            lead = STEP_STARTS.start[b.n] - VALUES.start[b.n]
                            used = lead + STEP_STARTS.events[b.n].index(start) + 1 - PROB_SLOTS
                            if VALUES.start[b.n] + used > 0:
                                act.wait_ge(prob_used, b.value(VALUES, used))
                            old = b.steps_back(STEP_STARTS, start, PROB_SLOTS)
                            if old is not None:
                                _, old_layer, old_g, old_s, _ = old
                                a = HPT * old_s + HPT - 1 if old_layer == 1 else max(1, old_s)
                                if old_layer == 1 or old_s < POOLED:
                                    at = ("values", old_layer, old_g, old_s if old_layer == 1 else a)
                                    act.wait_ge(added, b.last(ADDS, [("add", old_layer, old_g, a)], e, at))
                        act.wait_ge(score_full, b.after(SCORES, e))
                        act.activation(prob[STEP_STARTS.slot(b, start)][:, j, :],
                                       score_bank[(SCORES.rank[b.n][e] - 1) % SCORE_BANKS], ACT.Exp,
                                       scale=1.0 if layer == 1 else SCALE).then_inc(exp_done, 1)

            run(act, program, [GROUPS, NORMS, STORES, SIDE, STACKED[0], STACKED[1], SOFTMAX0, SCORES, VALUES, ADDS])

        @block.vector
        def _(dve):
            dve.wait_ge(loaded, 16 * N_LOADS)
            dve.memset(ones[:, :], 1.0).then_inc(set_up, 1)
            dve.memset(half_power[:, :], -0.5).then_inc(set_up, 1)
            dve.memset(count_n[:, :], float(N)).then_inc(set_up, 1)
            dve.wait_ge(biased, 1)
            dve.tensor_tensor(projb2[:, :], side_bank[:, 0:T], col("proj2_b"), ALU.add).then_inc(biased, 1)

            def program(b, number):
                for e in b.plan:
                    steps = [0]

                    def own(ins):
                        steps[0] += 1
                        ins.then_inc(vstep, 1)
                        dve.wait_ge(vstep, b.after(VSTEPS, e, own_steps(e) - steps[0]))

                    if e[0] == "stats":
                        _, layer, t, i = e
                        if layer == 0 and (t, i) == (0, 0):
                            dve.wait_ge(x_loaded, b.after(LOADS_X, ("load",)))
                        dve.bn_stats(stats[:, t, i, :], images[layer][:, t, i * QW:(i + 1) * QW]).then_inc(vstep, 1)
                        steps[0] += 1
                    elif e[0] == "norm":
                        layer = e[1]
                        dve.wait_ge(vstep, b.after(VSTEPS, ("stats", layer, T - 1, NQ - 1)))
                        dve.sem_inc(turned, 1)
                        for t in range(T):
                            ins = dve.bn_aggr(mv[:, t, :], stats[:, t, :, :].rearrange("p a s -> p (a s)"))
                        own(ins)
                        own(dve.tensor_tensor(small[:, :], mv[:, :, 0], mv[:, :, 0], ALU.mult))
                        dve.tensor_tensor(mv[:, :, 1], mv[:, :, 1], small[:, :], ALU.add).then_inc(moments_ready, 1)
                    elif e[0] == "affine":
                        layer = e[1]
                        dve.wait_ge(rstd_ready, b.after(NORMS, ("norm", layer)))
                        if NORMS.start[b.n] + NORMS.rank[b.n][("norm", layer)] > 1:
                            dve.wait_ge(h_ready, b.after(NORMS, ("norm", layer), 1))
                        own(dve.tensor_tensor(ga[:, :], rstd[:, :], col(f"gn{layer}_scale"), ALU.mult))
                        own(dve.tensor_tensor(small[:, :], gm[:, :, 0], ga[:, :], ALU.mult))
                        own(dve.tensor_tensor(gb[:, :], col(f"gn{layer}_bias"), small[:, :], ALU.subtract))
                        if layer == 0:
                            own(dve.tensor_tensor(small[:, :], mv[:, :, 0], ga[:, :], ALU.mult))
                            own(dve.tensor_tensor(small[:, :], small[:, :], gb[:, :], ALU.add))
                            own(dve.tensor_scalar(hsum[:, :], small[:, :], float(N), None, ALU.mult))
                        dve.sem_inc(affine_ready, 1)
                    elif e[0] == "softmax0":
                        dve.wait_ge(side_full, b.after(SIDE, ("side", 0, "logits")))
                        logits = side_bank[:, 0:T * DH].rearrange("p (t d) -> p t d", t=T)
                        own(dve.tensor_reduce(l0max[:, :], logits, AX_X, ALU.max))
                        dve.tensor_tensor(l0[:, :, :], logits, l0max[:, :].unsqueeze(2).broadcast_to([P, T, DH]),
                                          ALU.subtract).then_inc(l0_ready, 1)
                        dve.wait_ge(l0_ready, b.after(SOFTMAX0, e))
                        dve.sem_inc(side_free, 1)
                        dve.wait_ge(l0_exp, b.after(SOFTMAX0, e))
                        own(dve.tensor_reduce(l0sum[:, :], l0[:, :, :], AX_X, ALU.add))
                        own(dve.reciprocal(l0sum[:, :], l0sum[:, :]))
                        own(dve.tensor_tensor(l0[:, :, :], l0[:, :, :],
                                              l0sum[:, :].unsqueeze(2).broadcast_to([P, T, DH]), ALU.mult))
                        dve.transpose(l0T[:, :, :].rearrange("p t d -> p (t d)"),
                                      l0[:, :, :].rearrange("p t d -> p (t d)")).then_inc(l0T_ready, 1)
                    elif e[0] == "side":
                        layer, what = e[1], e[2]
                        if what == "mean":
                            dve.wait_ge(side_full, b.after(SIDE, e))
                            dve.tensor_copy(gm[:, :, :].rearrange("p t s -> p (t s)"),
                                            side_bank[:, 0:2 * T]).then_inc(side_free, 1)
                            dve.wait_ge(side_free, b.after(SIDE, e))
                            own(dve.tensor_tensor(small[:, :], gm[:, :, 0], gm[:, :, 0], ALU.mult))
                            dve.scalar_tensor_tensor(gvar[:, :], gm[:, :, 1], EPS, small[:, :], ALU.add,
                                                     ALU.subtract).then_inc(var_ready, 1)
                        elif what == "attb":
                            dve.wait_ge(side_full, b.after(SIDE, e))
                            dve.tensor_copy(attb[:, :], side_bank[:, 0:T]).then_inc(side_free, 1)
                        elif what == "projb":
                            dve.wait_ge(side_full, b.after(SIDE, e))
                            dve.tensor_tensor(projb0[:, :], side_bank[:, 0:T], col("proj0_b"),
                                              ALU.add).then_inc(side_free, 1)
                        elif what == "qk":
                            dve.wait_ge(hi_ready, b.after(PIECES, e))
                            m, i = e[3], e[4]
                            if layer == 1:
                                dve.tensor_tensor(lo[i][0:2 * HC1, :], side_bank[0:2 * HC1, :],
                                                  hi[i][0:2 * HC1, :].bitcast(F32), ALU.subtract).then_inc(lo_ready, 1)
                            else:
                                bias = col(("bq2", "bk2")[m % 2], m // 2) if layer == 2 else 0.0
                                dve.scalar_tensor_tensor(lo[i][:, :], side_bank, bias, hi[i][:, :].bitcast(F32),
                                                         ALU.add, ALU.subtract).then_inc(lo_ready, 1)
                            dve.wait_ge(lo_ready, b.after(PIECES, e))
                            dve.sem_inc(side_free, 1)
                        elif what == "out":
                            i = e[3]
                            t, part = i // NQ, slice((i % NQ) * QW, (i % NQ + 1) * QW)
                            if layer == 2 and i == 0:
                                dve.wait_ge(reloaded, b.after(RELOADS, ("reload",)))
                            dve.wait_ge(side_full, b.after(SIDE, e))
                            if layer == 0:
                                ins = dve.scalar_tensor_tensor(xa[:, t, part], side_bank, projb0[:, t:t + 1],
                                                               xa[:, t, part], ALU.add, ALU.add)
                            elif layer == 1:
                                ins = dve.scalar_tensor_tensor(xa[:, t, part], side_bank, col("gamma1", 0),
                                                               xa[:, t, part], ALU.mult, ALU.add)
                            elif layer == 2:
                                ins = dve.scalar_tensor_tensor(xb[:, t, part], side_bank, projb2[:, t:t + 1],
                                                               xb[:, t, part], ALU.add, ALU.add)
                            else:
                                ins = dve.scalar_tensor_tensor(hb[:, t, part], side_bank, col("proj3_b", t),
                                                               hb[:, t, part], ALU.add, ALU.add)
                            ins.then_inc(side_free, 1)
                            if i == T * NQ - 1:
                                dve.wait_ge(side_free, b.after(SIDE, e))
                    elif e[0] == "max":
                        _, layer, g, a = e
                        dve.wait_ge(max_full, b.after(MAXES, e))
                        bank = max_bank[(MAXES.rank[b.n][e] - 1) % MAX_BANKS]
                        dve.tensor_reduce(maxpart[layer][:, a // NQ, a % NQ:a % NQ + 1], bank, AX_X,
                                          ALU.max).then_inc(max_free, 1)
                    elif e[0] == "maxrow":
                        _, layer, g = e
                        n = MAXIMA[layer] // NQ
                        dve.wait_ge(max_free, b.after(MAXES, ("max", layer, g, MAXIMA[layer] - 1)))
                        own(dve.tensor_reduce(negmax[:, 0:n], maxpart[layer][:, 0:n, :], AX_X, ALU.max, negate=True))
                        rows = b.last(SIDE, [x for plan in PLANS for x in plan if x[0] == "maxrow"], e)
                        if rows is not None:
                            dve.wait_ge(side_free, rows)
                        own(dve.tensor_copy(maxsplit[:, 0:n, 0], negmax[:, 0:n]))
                        dve.tensor_tensor(maxsplit[:, 0:n, 1], negmax[:, 0:n], maxsplit[:, 0:n, 0],
                                          ALU.subtract).then_inc(maxsplit_ready, 1)
                    elif e[0] == "divide":
                        _, layer, g, i = e
                        part = slice(i * P, (i + 1) * P)
                        dst = (att1 if layer == 1 else att[:, g // NQ, :])[:, (g % NQ) * QW:(g % NQ + 1) * QW]
                        if i == 0:
                            dve.wait_ge(evacuated, b.last(GROUPS, [("finish", layer, g)], e))
                        own(dve.reciprocal(rsum[:, part], sums_bank[:, part]))
                        ins = dve.tensor_tensor(dst[:, part], dst[:, part], rsum[:, part], ALU.mult)
                        if i == QT - 1:
                            ins.then_inc(group_done, 1)
                    assert steps[0] == own_steps(e), (e, steps)

            run(dve, program, [LOADS_X, VSTEPS, NORMS, SIDE, SOFTMAX0, PIECES, RELOADS, MAXES, GROUPS])

        @block.tensor
        def _(pe):
            pe.wait_ge(loaded, 16 * N_LOADS)
            pe.wait_ge(set_up, 4)
            pe.wait_ge(kones, 1 + 2 * HEADS)
            for ot in range(T):
                for t in range(T):
                    ins = pe.matmul(side_bank[:, ot:ot + 1], wp_sb[2][:, t, ot * P:(ot + 1) * P], col("bv2", t),
                                    start=(t == 0), stop=(t == T - 1))
            ins.then_inc(biased, 1)
            pe.wait_ge(biased, 2)
            ident = const_sb[:, IDENT:IDENT + P]

            def program(b, number):
                for e in b.plan:
                    if e[0] in ("side", "maxrow"):
                        pe.wait_ge(side_free, b.after(SIDE, e, 1))
                    if e[0] == "side":
                        layer, what = e[1], e[2]
                        if what == "mean":
                            pe.wait_ge(moments_ready, b.after(NORMS, ("norm", layer)))
                            mean = MEAN8 if layer == 0 else MEAN32
                            ins = pe.matmul(side_bank[:, 0:2 * T], const_sb[:, mean:mean + P],
                                            mv[:, :, :].rearrange("p t s -> p (t s)"), start=True, stop=True)
                        elif what == "rows":
                            pe.wait_ge(h_ready, b.after(NORMS, ("norm", 0)))
                            for t in range(T):
                                pe.matmul(side_bank[0:1, t * P:(t + 1) * P], hsum[:, t:t + 1], ident,
                                          start=True, stop=True)
                            for t in range(T):
                                pe.matmul(side_bank[0:1, C:2 * C], hsum[:, t:t + 1], wqk0_sb[:, t, C:2 * C],
                                          start=(t == 0), stop=False)
                            ins = pe.matmul(side_bank[0:1, C:2 * C], count_n[:, :], rows0_sb[:, C:2 * C],
                                            start=False, stop=True)
                        elif what == "turn":
                            for a in range(2):
                                for t in range(T):
                                    kt = 2 * e[3] + a
                                    ins = pe.transpose(side_bank[:, a * C + t * P:a * C + (t + 1) * P],
                                                       ha[:, t, kt * P:(kt + 1) * P], ident)
                        elif what == "gram":
                            for t in range(T):
                                for kt in range(KC):
                                    ins = pe.matmul(side_bank[:, t * C:(t + 1) * C], hT[:, kt, t * P:(t + 1) * P],
                                                    hT[:, kt, :], start=(kt == 0), stop=(kt == KC - 1))
                        elif what == "keys":
                            for it in range(T):
                                dst = side_bank[:, it * C:(it + 1) * C]
                                for t in range(T):
                                    pe.matmul(dst, gram[:, t, it * P:(it + 1) * P], wqk0_sb[:, t, C:2 * C],
                                              start=(t == 0), stop=False)
                                ins = pe.matmul(dst, su_rows[:, it * P:(it + 1) * P], rows0_sb[:, C:2 * C],
                                                start=False, stop=True)
                        elif what == "logits":
                            for t in range(T):
                                for j in range(HPT):
                                    ch = slice((HPT * t + j) * DH, (HPT * t + j + 1) * DH)
                                    dst = side_bank[head_rows(j), t * DH:(t + 1) * DH]
                                    for k in range(T):
                                        pe.matmul(dst, wqk0_sb[:, k, ch], gk[:, k, ch], start=(k == 0), stop=False,
                                                  tile_position=(0, DH * j))
                                    ins = pe.matmul(dst, rows0_sb[:, ch], su_rows[:, C + ch.start:C + ch.stop],
                                                    start=False, stop=True, tile_position=(0, DH * j))
                        elif what == "attv":
                            pe.wait_ge(l0T_ready, b.after(SOFTMAX0, ("softmax0",)))
                            pe.sem_inc(turned, 1)
                            for t in range(T):
                                for j in range(HPT):
                                    r = head_rows(j)
                                    ins = pe.matmul(side_bank[r, t * C:(t + 1) * C], l0T[r, t, :], wv0_sb[r, t, :],
                                                    start=True, stop=True, tile_position=(DH * j, DH * j))
                        elif what == "attb":
                            pe.sem_inc(turned, 1)
                            for t in range(T):
                                for j in range(HPT):
                                    r = head_rows(j)
                                    ins = pe.matmul(side_bank[r, t:t + 1], l0T[r, t, :], col("bv0", t)[r, :],
                                                    start=True, stop=True, tile_position=(DH * j, DH * j))
                        elif what == "projb":
                            for ot in range(T):
                                for t in range(T):
                                    ins = pe.matmul(side_bank[:, ot:ot + 1], wp_sb[0][:, t, ot * P:(ot + 1) * P],
                                                    attb[:, t:t + 1], start=(t == 0), stop=(t == T - 1))
                        elif what == "mix":
                            for it in range(T):
                                for t in range(T):
                                    ins = pe.matmul(side_bank[:, it * C:(it + 1) * C],
                                                    attv[:, t, it * P:(it + 1) * P], wp_sb[0][:, t, :],
                                                    start=(t == 0), stop=(t == T - 1))
                        elif what == "qk":
                            m, i = e[3], e[4]
                            part = slice(i * QW, (i + 1) * QW)
                            if layer == 1:
                                for t in range(T):
                                    ins = pe.matmul(side_bank[0:2 * HC1, :], wa1_sb[:, t, 0:2 * HC1], xa[:, t, part],
                                                    start=(t == 0), stop=(t == T - 1))
                            else:
                                if m == 0 and i == 0:
                                    pe.wait_ge(h_ready, b.after(NORMS, ("norm", layer)))
                                o = (m % 2) * C + (m // 2) * P
                                for t in range(T):
                                    ins = pe.matmul(side_bank, wqkv_sb[layer][:, t, o:o + P],
                                                    normed[layer][:, t, part], start=(t == 0), stop=(t == T - 1))
                        elif what == "v":
                            per, width = (KC // 2, VC1) if layer == 1 else (2, C)
                            src, w, o = (xa, wa1_sb, 2 * HC1) if layer == 1 else (normed[layer], wqkv_sb[layer], 2 * C)
                            for a in range(per):
                                kt = per * e[3] + a
                                for t in range(T):
                                    ins = pe.matmul(side_bank[:, a * width:(a + 1) * width],
                                                    src[:, t, kt * P:(kt + 1) * P], w[:, t, o:o + width],
                                                    start=(t == 0), stop=(t == T - 1))
                        elif what == "out":
                            i = e[3]
                            ot, part = i // NQ, slice((i % NQ) * QW, (i % NQ + 1) * QW)
                            if layer != 0 and i == 0:
                                g = NQ - 1 if layer == 1 else T * NQ - 1
                                pe.wait_ge(group_done, b.last(GROUPS, [("finish", layer, g)], e))
                            if layer == 1:
                                ins = pe.matmul(side_bank, wo1_sb[:, ot * P:(ot + 1) * P], att1[:, part],
                                                start=True, stop=True)
                            else:
                                w, src = (mixT, ha) if layer == 0 else (wp_sb[layer], att)
                                for t in range(T):
                                    ins = pe.matmul(side_bank, w[:, t, ot * P:(ot + 1) * P], src[:, t, part],
                                                    start=(t == 0), stop=(t == T - 1))
                        ins.then_inc(side_full, 1)
                    elif e[0] == "max":
                        _, layer, g, a = e
                        r = MAXES.rank[b.n][e]
                        if MAXES.start[b.n] + r > MAX_BANKS:
                            pe.wait_ge(max_free, b.after(MAXES, e, MAX_BANKS))
                        half = slice((a % NQ) * QW, (a % NQ + 1) * QW)
                        if a == 0 and (layer == 1 and g == 0 or layer != 1 and g % NQ == 0):
                            ms = [0] if layer == 1 else [g // NQ * 2, g // NQ * 2 + 1]
                            for i in range(2):
                                pe.wait_ge(stacked[i], b.last(STACKED[i], [("stack", layer, m, i) for m in ms], e))
                        if layer == 1:
                            q = (g * QT + a // NQ) * P
                            left, right = Q1[0:SPLIT, q:q + P], K1[0:SPLIT, half]
                        else:
                            t, qc = g // NQ, g % NQ
                            qt, j = a // NQ // HPT, a // NQ % HPT
                            q = (qc * QT + qt) * P
                            left, right = Q[0:SPLIT, HPT * t + j, q:q + P], K[0:SPLIT, HPT * t + j, half]
                        pe.matmul(max_bank[(r - 1) % MAX_BANKS], left, right, start=True, stop=True).then_inc(max_full, 1)
                    elif e[0] == "maxrow":
                        _, layer, g = e
                        pe.wait_ge(maxsplit_ready, b.after(MAXROWS, e))
                        w = 1 if layer == 1 else HPT
                        for qt in range(QT):
                            ins = pe.matmul(side_bank[MAXROW:MAXROW + 2 * w, qt * P:(qt + 1) * P],
                                            maxsplit[:, qt * w:(qt + 1) * w, :].rearrange("p j s -> p (j s)"),
                                            ident_bf[:, :], start=True, stop=True, tile_position=(0, MAXROW))
                        ins.then_inc(side_full, 1)
                    elif e[0] == "score":
                        _, layer, g, s, j = e
                        r = SCORES.rank[b.n][e]
                        if r > SCORE_BANKS:
                            pe.wait_ge(exp_done, b.after(SCORES, e, SCORE_BANKS))
                        elif SCORES.start[b.n]:
                            pe.wait_ge(exp_done, b.before(SCORES))
                        if s == 0 and j == 0:
                            pe.wait_ge(side_free, b.last(SIDE, [("maxrow", layer, g)], e))
                        if layer == 1:
                            kt = HPT * s + j
                            left, right = K1[0:MAXROW + 2, kt * P:(kt + 1) * P], Q1[0:MAXROW + 2, g * QW:(g + 1) * QW]
                        else:
                            t, qc = g // NQ, g % NQ
                            left = K[0:ROWS, HPT * t + j, s * P:(s + 1) * P]
                            right = Q[0:ROWS, HPT * t + j, qc * QW:(qc + 1) * QW]
                        pe.matmul(score_bank[(r - 1) % SCORE_BANKS], left, right,
                                  start=True, stop=True).then_inc(score_full, 1)
                    elif e[0] in ("value", "values"):
                        layer, g, s = e[1:4]
                        j = e[4] if e[0] == "value" else HPT - 1
                        slot = prob[VALUES.slot(b, ("values", layer, g, s))]
                        if s == 0 and j == 0 and GROUPS.start[b.n] + GROUPS.events_before(b, e):
                            pe.wait_ge(evacuated, b.until(GROUPS, e))
                        pe.wait_ge(exp_done, b.last(SCORES, [("score", layer, g, s, j)], e))
                        if layer == 1:
                            kt = HPT * s + j
                            ins = pe.matmul(values_bank, vT1[:, kt, :], slot[:, j, :],
                                            start=(kt == 0), stop=(kt == KC - 1))
                        else:
                            head = HPT * (g // NQ) + j
                            ins = pe.matmul(values_bank[head_rows(j), :], vT[layer][:, s, head * DH:(head + 1) * DH],
                                            slot[:, j, :], start=(s == 0), stop=(s == KC - 1),
                                            tile_position=(0, DH * j))
                        if e[0] == "values":
                            if layer != 1 and s >= POOLED:
                                if s == POOLED and GROUPS.start[b.n] + GROUPS.events_before(b, e):
                                    pe.wait_ge(group_done, b.until(GROUPS, e))
                                for j in range(HPT):
                                    ins = pe.matmul(sums_bank[head_rows(j), :], ones[:, 0:DH], slot[:, j, :],
                                                    start=(s == POOLED), stop=False, tile_position=(0, DH * j))
                            ins.then_inc(prob_used, 1)
                    elif e[0] == "finish":
                        _, layer, g = e
                        add = ("add", layer, g, (KC if layer == 1 else POOLED) - 1)
                        at = ("values", layer, g, STEPS[1] - 1 if layer == 1 else POOLED - 1)
                        pe.wait_ge(added, b.last(ADDS, [add], e, at))
                        if (layer == 1 or POOLED == KC) and GROUPS.start[b.n] + GROUPS.events_before(b, e):
                            pe.wait_ge(group_done, b.until(GROUPS, e))
                        if layer == 1:
                            ins = pe.matmul(sums_bank, ones[:, :], acc[:, 0, :], start=True, stop=True)
                        else:
                            for j in range(HPT):
                                ins = pe.matmul(sums_bank[head_rows(j), :], ones[:, 0:DH], acc[:, j, :],
                                                start=(POOLED == KC), stop=True, tile_position=(0, DH * j))
                        ins.then_inc(values_done, 1)

            run(pe, program, [SIDE, NORMS, SOFTMAX0, GROUPS, MAXES, STACKED[0], STACKED[1], MAXROWS, SCORES, ADDS])


def kernel(**inputs):
    import numpy as np
    import concourse.bacc as bacc
    from concourse.bass_utils import run_bass_kernel_spmd

    a = {k: np.asarray(v) for k, v in inputs.items()}

    def column(v):
        return v.reshape(T, P).T

    def beside(v):
        return v.reshape(T, HPT, DH, -1).transpose(0, 2, 1, 3).reshape(v.shape)

    def qkv(w):
        return np.concatenate([beside(w[:C]), beside(w[C:2 * C]), w[2 * C:]]).T

    cols = [a["L0_conv_gn_scale"], a["L0_conv_gn_bias"], a["L0_conv_qkv_b"][2 * C:], a["L0_conv_proj_b"],
            a["L2_conv_gn_weight"], a["L2_conv_gn_bias"], beside(a["L2_conv_qkv_bias"][:C]),
            beside(a["L2_conv_qkv_bias"][C:2 * C]), a["L2_conv_qkv_bias"][2 * C:], a["L2_conv_proj_bias"],
            a["L3_conv_gamma"], a["L3_conv_beta"], a["L3_conv_b_out"], np.broadcast_to(a["L1_conv_gamma"], (C,))]
    consts = np.zeros((P, CONST_COLS), np.float32)
    for i in range(P):
        consts[i, IDENT + i] = 1.0
        for at, width in ((MEAN8, C // 32), (MEAN32, C // 8)):
            consts[i, at + i // width * width:at + (i // width + 1) * width] = 1.0 / width
    arrays = {
        "x": a["x"].reshape(B, C, N),
        "wqk0T": a["L0_conv_qkv_w"][:2 * C].T, "wv0": a["L0_conv_qkv_w"][2 * C:], "wp0T": a["L0_conv_proj_w"].T,
        "rows0": a["L0_conv_qkv_b"][:2 * C].reshape(1, 2 * C),
        "waT1": a["L1_conv_Wa"].T, "woT1": a["L1_conv_Wo"].T,
        "wqkv2T": qkv(a["L2_conv_qkv_weight"]), "wp2T": a["L2_conv_proj_weight"].T,
        "wqkv3T": qkv(a["L3_conv_w_qkv"]), "wp3T": a["L3_conv_w_out"].T,
        "cols": np.concatenate([column(v) for v in cols], axis=1), "consts": consts,
    }
    arrays = {k: np.ascontiguousarray(v) for k, v in arrays.items()}
    nc = bacc.Bacc("TRN2", target_bir_lowering=False, num_devices=1)
    args = {k: nc.dram_tensor(f"in_{k}", v.shape, F32, kind="ExternalInput").ap() for k, v in arrays.items()}
    scratch = nc.dram_tensor("scratch", (B, C, N), F32, kind="Internal").ap()
    out = nc.dram_tensor("out_0", (B, C, N), F32, kind="ExternalOutput").ap()
    build(nc, **args, scratch=scratch, out=out)
    r = run_bass_kernel_spmd(nc, [{f"in_{k}": v for k, v in arrays.items()}], core_ids=[0])
    return r.results[0]["out_0"].reshape(B, C, 32, 32)
```

```python
from contextlib import ExitStack

import concourse.bass as bass
from concourse import mybir

F32 = mybir.dt.float32
F32R = mybir.dt.float32r
BF16 = mybir.dt.bfloat16
ALU = mybir.AluOpType
ACT = mybir.ActivationFunctionType
AX_X = mybir.AxisListType.X

P = 128
B = 8
C = 256
N = 1024
T = C // P
HEADS = 8
DH = C // HEADS
HPT = P // DH
QW = 512
NQ = N // QW
KC = N // P
QT = QW // P
HC1 = 32
VC1 = C // 2
EPS = 1e-5
SCALE = float(DH) ** -0.5
SPLIT = 3 * DH
MAXROW = SPLIT
ROWS = MAXROW + 2 * HPT
SCORE_BANKS = 2
MAX_BANKS = 3
SIDE_BANKS = 2
PROB_SLOTS = 4
POOLED = 8
STEPS = {1: KC // HPT, 2: KC, 3: KC}
MAXIMA = {1: QT * NQ, 2: HPT * QT * NQ, 3: HPT * QT * NQ}
LAG = 2 * HPT
DIVIDE_EVERY = 2
AFTER_FINISH = 17
KEYS_BY = 29
LAST_PIECE = 30
START_MAX = 1
FIRST_MAX = 14
ROW_GAP = 2
ROW_SLOTS = 6
MOST_MAXIMA = 3
AHEAD = 3
BEHIND = 4
PIECE_AHEAD = 2

COLS = {name: T * i for i, name in enumerate(
    ["gn0_scale", "gn0_bias", "bv0", "proj0_b", "gn2_scale", "gn2_bias", "bq2", "bk2", "bv2", "proj2_b",
     "gn3_scale", "gn3_bias", "proj3_b", "gamma1"])}
IDENT, MEAN8, MEAN32, ZERO = 0, P, 2 * P, 3 * P
CONST_COLS = 3 * P + T



def normalise(layer):
    return ([("stats", layer, t, i) for t in range(T) for i in range(NQ)]
            + [("norm", layer), ("side", layer, "mean"), ("power", layer), ("affine", layer)]
            + [("apply", layer, t, i) for t in range(T) for i in range(NQ)])


def split_operand(layer, m):
    return [x for i in range(NQ) for x in (("side", layer, "qk", m, i), ("stack", layer, m, i))]


def side(layer, what, n):
    return [("side", layer, what, i) for i in range(n)]


def channel_attention(first):
    if first:
        return (normalise(0) + side(0, "rows", 2) + side(0, "turn", KC // 2))
    return ([("side", 0, "gram"), ("side", 0, "keys"), [("side", 0, "logits"), ("softmax0",)]]
            + [("side", 0, x) for x in ("attv", "attb", "projb", "mix")] + side(0, "out", T * NQ))


def before_layer1():
    return split_operand(1, 0) + side(1, "v", 2)


def after_layer1(rest=True):
    more = split_operand(2, 0) + split_operand(2, 1) + side(2, "v", KC // 2)
    return side(1, "out", T * NQ) + [("save",)] + normalise(2) + (more if rest else [])


def chunks(piece):
    if piece[0] != "side":
        return 1
    return {"qk": T, "v": T, "out": 1 if piece[1] == 1 else T, "gram": KC, "keys": T, "mix": T}.get(piece[2], 1)


def cut(pieces):
    return [x for piece in pieces for x in [("begin", c) + piece[1:] for c in range(chunks(piece) - 1)] + [piece]]


def spread(first, last, pieces):
    pieces = cut(pieces)
    return [(first + (last - first) * (2 * i + 1) // (2 * len(pieces)), x) for i, x in enumerate(pieces)]


def group_sequence():
    after = AFTER_FINISH
    end = LAST_PIECE
    slots = KC * HPT
    late2_qk = split_operand(2, 2) + split_operand(2, 3)
    out3 = side(3, "out", T * NQ) + [("store",)]
    late2 = [(2, 0, spread(0, after, late2_qk[:4]) + spread(after, end, late2_qk[4:] + out3))]
    late2_first = [(2, 0, spread(0, end, late2_qk))]

    def layer2(prior, following):
        q3 = split_operand(3, 0) + split_operand(3, 1) if prior else []
        a = [(0, ("load",))] if following else []
        if prior:
            a += zip((1, 2, 3, 4, 5, 8, 13, 15, 17, 18, 19, 20), normalise(3))
            early = [x for x in q3[:4] if x[0] == "side"]
            q3 = [x for x in q3 if x not in early]
            a += spread(22, end, early)
        a.append((21, ("reload",)))
        late = []
        if following:
            a += zip((10, 12, 14, 16, 17, 20, 26, 27), normalise(0))
            late = [*zip((0, 1, 2, 3), normalise(0)[-T * NQ:])]
        turned = (side(0, "rows", 2) + side(0, "turn", KC // 2)) if following else []
        v3 = side(3, "v", KC // 2) if prior else []
        c = channel_attention(False) if following else []
        more = spread(4, KEYS_BY, q3[2:4] + turned + c[:3] + q3[4:])
        return [(2, 1, a), (2, 2, [(0, x) for x in q3[:2]] + late + more), (2, 3, spread(0, end, c[3:] + v3))]

    out2 = side(2, "out", T * NQ)
    layer1 = [(1, 0, []), (1, 1, [])]
    q3 = split_operand(3, 2) + split_operand(3, 3)
    early3 = [x for x in q3[:4] if x[0] == "side"]
    out1 = after_layer1(False)

    def gap(pieces):
        return (None, None, pieces)

    first = ([gap([("load",)] + channel_attention(True) + channel_attention(False) + before_layer1())] + layer1
             + [gap(after_layer1())] + late2_first)
    second = layer2(False, True) + [gap(out2 + before_layer1())] + layer1 + [gap(after_layer1())] + late2_first
    steady = (layer2(True, True)
              + [(3, 0, spread(0, 12, before_layer1()) + spread(after, end, out2),
                  [(3, 1, 12, 0, 12), (1, 0, 8, 14, 21), (1, 0, None, 22, 22), (1, 1, 8, 23, 29)]),
                 (1, 0, [], [(1, 1, None, 2, 2), (3, 1, 10, 0, 7)]),
                 (1, 1, spread(0, 6, early3), [(3, 1, 10, 0, 4), (3, 1, None, 6, 6)]),
                 (3, 1, spread(0, 12, [x for x in q3 if x not in early3])
                  + spread(after, end, out1[:T * NQ + 1]),
                  [(3, 2, 32, FIRST_MAX, slots - 7), (3, 2, None, slots - 5, slots - 5)]),
                 (3, 2, [*zip((0, 1, 2, 3, 4, 9, 10, 15, 17, 18, 19, 20), out1[T * NQ + 1:])]
                  + spread(20, KEYS_BY, split_operand(2, 0) + split_operand(2, 1))),
                 (3, 3, spread(0, end, side(2, "v", KC // 2)))] + late2)
    rest3 = [(3, 1, []), (3, 2, []), (3, 3, []), gap(out3)]
    last2 = layer2(True, False) + [(3, 0, spread(0, after, q3[:4]) + spread(after, end, out2 + q3[4:]))] + rest3
    last3 = ([gap(normalise(3) + split_operand(3, 0) + split_operand(3, 1) + side(3, "v", KC // 2)),
              (3, 0, spread(0, end, q3))] + rest3)
    return [first, second, steady, last2, last3]


RUNS = [1, 1, B - 2, 1, 1]
STEADY = 2


def flat(pieces):
    return [x for piece in pieces for x in (piece if isinstance(piece, list) else [piece])]


class Load:

    HAND_OVER = 1.0

    def __init__(self):
        self.tensor = self.vector = self.scalar = 0.0
        self.exps, self.maxes = [0.0] * SCORE_BANKS, [0.0] * MAX_BANKS

    def product(self, length):
        self.tensor += length
        return self.tensor + self.HAND_OVER

    def on_scalar(self, ready, length):
        self.scalar = max(self.scalar, ready) + length
        return self.scalar

    def on_vector(self, ready, length):
        self.vector = max(self.vector, ready) + length
        return self.vector

    def room(self):
        return self.maxes[-MAX_BANKS] <= self.tensor

    def add(self, e):
        kind = e[0]
        if kind == "score":
            self.tensor = max(self.tensor, self.exps[-SCORE_BANKS] + self.HAND_OVER / 2)
            self.exps.append(self.on_scalar(self.product(1), 2.2))
        elif kind == "max":
            self.tensor = max(self.tensor, self.maxes[-MAX_BANKS] + self.HAND_OVER / 2)
            self.maxes.append(self.on_vector(self.product(1), 3.0))
        elif kind in ("value", "values"):
            self.product(4 if e[1] == 1 else 1)
        elif kind == "finish":
            self.product(2)
        elif kind == "evacuate":
            self.on_scalar(self.tensor + self.HAND_OVER, 4.4)
        elif kind == "begin":
            self.product(4)
        elif kind == "side":
            what = e[2]
            ready = self.product({"mean": 0.2, "rows": 0.5, "turn": 2, "attb": 0.2, "projb": 0.2}.get(what, 4))
            if what in ("mean", "attb", "projb", "out"):
                self.on_vector(ready, 3 if what == "out" else 1)
            else:
                ready = self.on_scalar(ready, 2.4)
                if what == "qk":
                    self.on_vector(ready + self.HAND_OVER, 2.8)
        elif kind == "maxrow":
            self.on_scalar(self.product(0.4), 2.2)
        elif kind in ("stats", "divide", "split", "softmax0", "norm", "affine"):
            self.on_vector(self.tensor, {"stats": 2.8, "divide": 5, "split": 2, "softmax0": 6}.get(kind, 1.5))
        elif kind == "apply":
            self.on_scalar(self.tensor, 2.2)


def plans():
    out = []
    late = []
    divides = []
    load = Load()

    def close(plan, pieces):
        while [x[0] for x in plan if x[0] in ("begin", "side")][-1:] == ["begin"]:
            plan += flat([pieces.pop(0)[1]])

    def advance(plan, pieces=()):
        x = late.pop(0)
        if x[0] == "values" and x[3] == STEPS[x[1]] - 1:
            close(plan, pieces)
        plan.append(x)
        if x[0] == "values" and x[3] == STEPS[x[1]] - 1:
            plan += [("finish",) + x[1:3], ("evacuate",) + x[1:3]]
            divides.extend(("divide",) + x[1:3] + (i,) for i in range(QT))

    turns = group_sequence()
    for n, groups in enumerate(turns):
        plan = []
        sought = {}
        counted = [0]

        def room():
            for e in plan[counted[0]:]:
                load.add(e)
            counted[0] = len(plan)
            return load.room()

        def seek(layer, g, count):
            first = sought.get((layer, g), 0)
            sought[layer, g] = first + count
            return [("max", layer, g, a) for a in range(first, first + count)]

        def starved(piece, slot):
            room()
            return (piece[0] <= slot + PIECE_AHEAD and piece[1][0] in ("begin", "side", "stack")
                    and piece[1][-1] != "mean" and load.exps[-SCORE_BANKS] > load.tensor + 1)

        for at, (layer, g, pieces, *maxima) in enumerate(groups):
            following = groups[at + 1] if at + 1 < len(groups) else turns[n + 1][0] if n + 1 < len(turns) else (None,)
            if layer is None:
                while late:
                    advance(plan)
                plan += divides + flat(cut(pieces))
                divides.clear()
                if following[0] is not None and at + 1 < len(groups):
                    plan += seek(*following[:2], MAXIMA[following[0]])
                    plan += [("split",) + following[:2], ("maxrow",) + following[:2]]
                continue
            slots = STEPS[layer] * HPT
            if maxima:
                maxima = maxima[0]
            elif following[0] is not None:
                rows_at = slots - ROW_SLOTS
                maxima = [following[:2] + (MAXIMA[following[0]], START_MAX if slots > KC else 0, rows_at - ROW_GAP),
                          following[:2] + (None, rows_at, rows_at)]
            pieces = sorted(pieces, key=lambda x: x[0])
            placed = {}
            for slot in range(slots):
                s, j = slot // HPT, slot % HPT
                plan.append(("score", layer, g, s, j))
                late.append(("values", layer, g, s) if j == HPT - 1 else ("value", layer, g, s, j))
                for to_layer, to_g, count, low, high in maxima:
                    if count is None:
                        if slot == low:
                            close(plan, pieces)
                            plan.append(("maxrow", to_layer, to_g))
                    elif low <= slot <= high:
                        due = count * (slot - low + 1) / (high - low + 1)
                        done = placed.get((to_layer, to_g), 0)
                        here = 0
                        while done < count and (slot == high or here < MOST_MAXIMA and done < due + AHEAD
                                             and (room() or done < due - BEHIND)):
                            plan += seek(to_layer, to_g, 1)
                            done, here = done + 1, here + 1
                        placed[to_layer, to_g] = done
                        if slot == high and sought[to_layer, to_g] == MAXIMA[to_layer]:
                            plan.append(("split", to_layer, to_g))
                if divides and slot % DIVIDE_EVERY == 0:
                    plan.append(divides.pop(0))
                while pieces and (pieces[0][0] <= slot or slot == slots - 1 or starved(pieces[0], slot)):
                    plan += flat([pieces.pop(0)[1]])
                while j == HPT - 1 and len(late) > LAG:
                    advance(plan, pieces)
        out.append(plan)
    assert not late and not divides
    return out


class Events:

    def __init__(self, all_plans, events_of, weight=lambda e: 1):
        self.rank, self.events, self.weight = [], [], weight
        for plan in all_plans:
            events = [x for e in plan for x in events_of(e)]
            self.events.append(events)
            rank, n = {}, 0
            for e in events:
                n += weight(e)
                rank[e] = n
            self.rank.append(rank)
        self.total = [sum(weight(e) for e in events) for events in self.events]
        self.start = [sum(self.total[j] * RUNS[j] for j in range(i)) for i in range(len(all_plans))]
        self.ahead = 0 if self.start[STEADY] else 1

    def number(self, turn, e):
        return self.start[turn.n] + self.events[turn.n].index(e)

    def events_before(self, turn, here):
        return sum(turn.place[e] < turn.place[here] for e in self.events[turn.n])

    def slot(self, turn, e):
        assert self.total[STEADY] % PROB_SLOTS == 0
        return self.number(turn, e) % PROB_SLOTS


class Turn:

    def __init__(self, eng, all_plans, n, used=()):
        self.eng, self.n, self.plan = eng, n, all_plans[n]
        self.place = {}
        for i, e in enumerate(self.plan):
            self.place[e] = i
        self.base, self.used = {}, set()
        if n == STEADY:
            name = eng.engine.name
            self.values = [eng.alloc_register(f"awaited{i}_{name}") for i in range(2)]
            for i, events in enumerate(used):
                self.base[events] = eng.alloc_register(f"before{i}_{name}")
                eng.reg_mov(self.base[events], events.start[n] + events.ahead)

    def value(self, events, more):
        if self.n != STEADY:
            return events.start[self.n] + events.ahead + more
        self.used.add(events)
        assert events in self.base, events.events[self.n][:3]
        if more == 0:
            return self.base[events]
        self.values.reverse()
        self.eng.reg_add(self.values[0], self.base[events], more)
        return self.values[0]

    def before(self, events):
        return self.value(events, 0)

    def after(self, events, e, less=0):
        return self.value(events, events.rank[self.n][e] - less)

    def until(self, events, here):
        n = sum(events.weight(e) for e in events.events[self.n] if self.place[e] < self.place[here])
        return self.value(events, n)

    def last(self, events, any_of, here, at=None):
        ranks = [events.rank[self.n][e] for e in any_of
                 if e in events.rank[self.n] and self.place[at or e] < self.place[here]]
        if ranks:
            return self.value(events, max(ranks))
        prior = [self.n - 1] + ([self.n] if self.n == STEADY else [])
        back = [events.total[i] - events.rank[i][e] for i in prior for e in any_of
                if i >= 0 and e in events.rank[i]]
        return self.value(events, -min(back)) if back else None

    def steps_back(self, starts, start, n):
        i = starts.events[self.n].index(start) - n
        if i >= 0:
            return starts.events[self.n][i]
        prior = [self.n - 1] + ([self.n] if self.n == STEADY else [])
        found = {starts.events[k][i] for k in prior if k >= 0}
        assert len(found) <= 1
        return found.pop() if found else None

    def end(self):
        assert self.used == set(self.base), [x.events[self.n][:2] for x in set(self.base) - self.used]
        for events, register in self.base.items():
            self.eng.reg_add(register, register, events.total[self.n])


def build(nc, x, wqk0T, wv0, wp0T, rows0, waT1, woT1, wqkv2T, wp2T, wqkv3T, wp3T, cols, consts, scratch, out):
    PLANS = plans()

    def when(test, weight=lambda e: 1):
        return Events(PLANS, lambda e: [e] if test(e) else [], weight)

    LOADS_X = when(lambda e: e[0] == "load", lambda e: 16)
    SAVES = when(lambda e: e[0] == "save", lambda e: 16)
    RELOADS = when(lambda e: e[0] == "reload", lambda e: 16)
    STORES = when(lambda e: e[0] == "store", lambda e: 16)
    SIDE = when(lambda e: e[0] in ("side", "maxrow", "finish"))
    assert SIDE.total[STEADY] % SIDE_BANKS == 0

    def bank_of(n, e):
        return (SIDE.start[n] + SIDE.rank[n][e] - 1) % SIDE_BANKS

    class SideEvents(Events):

        def __init__(self, bank):
            by_turn = [[e for e in SIDE.events[n] if bank_of(n, e) == bank] for n in range(len(PLANS))]
            super().__init__(by_turn, lambda e: [e])

    SIDES = [SideEvents(bank) for bank in range(SIDE_BANKS)]
    MAXES = when(lambda e: e[0] == "max")
    SCORES = when(lambda e: e[0] == "score")
    VALUES = when(lambda e: e[0] == "values")
    GROUPS = when(lambda e: e[0] == "finish")
    SPLITS = when(lambda e: e[0] == "split")
    ROWS_PLACED = when(lambda e: e[0] == "maxrow", lambda e: 16)
    NORMS = when(lambda e: e[0] == "norm")
    SOFTMAX0 = when(lambda e: e[0] == "softmax0")
    PIECES = when(lambda e: e[0] == "side" and e[2] == "qk")

    STEP_STARTS = when(lambda e: e[0] == "score" and e[4] == 0)

    def adds(e):
        if e[0] != "values":
            return []
        _, layer, g, s = e
        tiles = range(HPT * s, HPT * (s + 1)) if layer == 1 else [s]
        return [("add", layer, g, a) for a in tiles if a and (layer == 1 or a < POOLED)]

    ADDS = Events(PLANS, adds)
    STACKED = [Events(PLANS, lambda e, s=s: [e] if e[0] == "stack" and e[-1] % 2 == s else [],
                      lambda e: 16 * (6 if e[1] == 1 else 3)) for s in range(2)]
    OWN = {"stats": 1, "norm": 2, "softmax0": 4, "split": 2, "divide": 1}

    def own_steps(e):
        if e[0] == "affine":
            return 6 if e[1] == 0 else 3
        if e[0] == "side":
            return 1 if e[2] == "mean" else 0
        return OWN.get(e[0], 0)

    VSTEPS = when(own_steps, own_steps)

    ctx = ExitStack()
    with ctx:
        def sb(name, shape, dt=F32):
            return ctx.enter_context(nc.sbuf_tensor(name, shape, dt))

        def sem(name):
            return ctx.enter_context(nc.semaphore(name))

        wqk0_sb = sb("wqk0_sb", [P, T, 2 * C])
        wv0_sb = sb("wv0_sb", [P, T, C])
        wp_sb = {0: sb("wp0_sb", [P, T, C]), 2: sb("wp2_sb", [P, T, C]), 3: sb("wp3_sb", [P, T, C])}
        wa1_sb = sb("wa1_sb", [P, T, 2 * HC1 + VC1])
        wo1_sb = sb("wo1_sb", [P, C])
        wqkv_sb = {2: sb("wqkv2_sb", [P, T, 3 * C]), 3: sb("wqkv3_sb", [P, T, 3 * C])}
        rows0_sb = sb("rows0_sb", [1, 2 * C])
        cols_sb = sb("cols_sb", [P, len(COLS) * T])
        const_sb = sb("const_sb", [P, CONST_COLS])
        ident_bf = sb("ident_bf", [P, P], BF16)
        ones = sb("ones", [P, DH])
        half_power = sb("half_power", [P, T])
        count_n = sb("count_n", [1, 1])
        projb2 = sb("projb2", [P, T])

        xa = sb("xa", [P, T, N])
        xb = sb("xb", [P, T, N])
        ha = sb("ha", [P, T, N])
        hb = sb("hb", [P, T, N])
        images = {0: xa, 2: xa, 3: xb}
        normed = {0: ha, 2: ha, 3: hb}
        att = sb("att", [P, T, N])
        att1 = att[:, 1, :]
        vT2 = sb("vT2", [P, KC, C])
        vT3 = sb("vT3", [P, KC, C])
        hT = vT3
        stats = sb("stats", [P, T, NQ, 6])
        mv = sb("mv", [P, T, 2])
        gm = sb("gm", [P, T, 2])
        gvar = sb("gvar", [P, T])
        rstd = sb("rstd", [P, T])
        ga = sb("ga", [P, T])
        gb = sb("gb", [P, T])
        small = sb("small", [P, T])
        hsum = sb("hsum", [P, T])
        su_rows = att[0:1, 1, 0:2 * C]
        products0 = sb("products0", [P, 2, T, C])
        gram, gk = products0[:, 0], products0[:, 1]
        vT1 = products0[:, :, :, :].rearrange("p a t c -> p (a t c)").rearrange("p (k c) -> p k c", c=VC1)
        vT = {1: vT1, 2: vT2, 3: vT3}
        attv, mixT = gram, gk
        l0, l0T = (att[:, 1, a:a + T * DH].rearrange("p (t d) -> p t d", t=T) for a in (QW, QW + T * DH))
        l0max = sb("l0max", [P, T])
        l0sum = sb("l0sum", [P, T])
        attb = sb("attb", [P, T])
        projb0 = sb("projb0", [P, T])
        hi = [sb(f"hi{s}", [P, QW], F32R) for s in range(2)]
        lo = [sb(f"lo{s}", [P, QW], F32R) for s in range(2)]
        Q = sb("Q", [P, HEADS, N], F32R)
        K = sb("K", [P, HEADS, N], F32R)
        Q1, K1 = Q[:, HPT, :], K[:, HPT, :]
        maxpart = {layer: sb(f"maxpart{layer}", [P, QT * HPT, NQ]) for layer in (1, 2)}
        maxpart[3] = maxpart[2]
        negmax = sb("negmax", [P, QT * HPT])
        maxsplit = sb("maxsplit", [P, QT * HPT, 2], BF16)
        prob = [sb(f"prob{i}", [P, HPT, QW]) for i in range(PROB_SLOTS)]
        acc = sb("acc", [P, HPT, QW])
        max_rows = sb("max_rows", [P, QW], F32R)
        sums = sb("sums", [P, QW])

        psum = ctx.enter_context(nc.psum_tensor("psum", [P, 8, QW], F32))
        score_bank = [psum[:, i, :] for i in range(SCORE_BANKS)]
        max_bank = [psum[:, SCORE_BANKS + i, :] for i in range(MAX_BANKS)]
        values_bank = psum[:, 5, :]
        side_banks = [psum[:, 6 + i, :] for i in range(SIDE_BANKS)]

        loaded = sem("loaded")
        kones = sem("kones")
        set_up = sem("set_up")
        biased = sem("biased")
        x_loaded = sem("x_loaded")
        saved = sem("saved")
        reloaded = sem("reloaded")
        stored = sem("stored")
        vstep = sem("vstep")
        moments_ready = sem("moments_ready")
        var_ready = sem("var_ready")
        rstd_ready = sem("rstd_ready")
        affine_ready = sem("affine_ready")
        h_ready = sem("h_ready")
        side_fulls = [sem(f"side{i}_full") for i in range(SIDE_BANKS)]
        side_frees = [sem(f"side{i}_free") for i in range(SIDE_BANKS)]
        hi_ready = sem("hi_ready")
        lo_ready = sem("lo_ready")
        stacked = [sem("stacked0"), sem("stacked1")]
        l0_ready = sem("l0_ready")
        l0_exp = sem("l0_exp")
        l0T_ready = sem("l0T_ready")
        max_full = sem("max_full")
        max_free = sem("max_free")
        maxsplit_ready = sem("maxsplit_ready")
        rows_placed = sem("rows_placed")
        score_full = sem("score_full")
        exp_done = sem("exp_done")
        prob_used = sem("prob_used")
        added = sem("added")
        evacuated = sem("evacuated")
        group_done = sem("group_done")
        turned = sem("turned")
        NEEDS = {("side", 0, "gram"): ("side", 0, "turn", KC // 2 - 1), ("side", 0, "keys"): ("side", 0, "gram"),
                 ("side", 0, "logits"): ("side", 0, "keys"), ("side", 0, "projb"): ("side", 0, "attb"),
                 ("side", 0, "mix"): ("side", 0, "attv"), ("side", 0, "out", 0): ("side", 0, "mix"),
                 ("side", 1, "qk", 0, 0): ("side", 0, "out", T * NQ - 1)}
        block = ctx.enter_context(nc.Block())

        SEMAPHORES = [
            (x_loaded, LOADS_X), (saved, SAVES), (reloaded, RELOADS), (stored, STORES), (vstep, VSTEPS),
            (moments_ready, NORMS), (var_ready, NORMS), (rstd_ready, NORMS), (affine_ready, NORMS), (h_ready, NORMS),
            *zip(side_fulls, SIDES), *zip(side_frees, SIDES), (hi_ready, PIECES), (lo_ready, PIECES),
            (stacked[0], STACKED[0]), (stacked[1], STACKED[1]), (l0_ready, SOFTMAX0), (l0_exp, SOFTMAX0),
            (l0T_ready, SOFTMAX0), (max_full, MAXES), (max_free, MAXES), (maxsplit_ready, SPLITS),
            (rows_placed, ROWS_PLACED),
            (score_full, SCORES), (exp_done, SCORES), (prob_used, VALUES), (added, ADDS),
            (evacuated, GROUPS), (group_done, GROUPS)]

        def col(name, t=None):
            a = COLS[name]
            return cols_sb[:, a:a + T] if t is None else cols_sb[:, a + t:a + t + 1]

        def image(ap, b):
            return ap[b].rearrange("(t p) n -> p t n", p=P)

        LOADS = [(wqk0_sb, wqk0T), (wv0_sb, wv0), (wp_sb[0], wp0T), (wa1_sb, waT1), (wqkv_sb[2], wqkv2T),
                 (wp_sb[2], wp2T), (wqkv_sb[3], wqkv3T), (wp_sb[3], wp3T)]
        N_LOADS = len(LOADS) + 4

        def head_rows(j):
            return slice(DH * j, DH * (j + 1))

        def filled(b, e):
            bank = bank_of(b.n, e)
            return side_fulls[bank], b.after(SIDES[bank], e)

        def taken(b, e):
            bank = bank_of(b.n, e)
            return side_frees[bank], b.after(SIDES[bank], e)

        def run(eng, program, used):
            for n in range(len(PLANS)):
                b = Turn(eng, PLANS, n, used)
                if n == STEADY:
                    with eng.Fori(n - 1, n - 1 + RUNS[n]) as number:
                        program(b, number)
                        b.end()
                else:
                    program(b, sum(RUNS[:n]) - 1)

        @block.sync
        def _(sp):
            for semaphore, events in SEMAPHORES:
                if events.ahead:
                    sp.sem_inc(semaphore, events.ahead)
            for dst, src in LOADS:
                sp.dma_start(dst[:, :, :], src.rearrange("(t p) o -> p t o", p=P)).then_inc(loaded, 16)
            sp.dma_start(wo1_sb[:, :], woT1).then_inc(loaded, 16)
            sp.dma_start(rows0_sb[:, :], rows0).then_inc(loaded, 16)
            sp.dma_start(cols_sb[:, :], cols).then_inc(loaded, 16)
            sp.dma_start(const_sb[:, :], consts).then_inc(loaded, 16)

            def program(b, number):
                for e in b.plan:
                    if e[0] == "load":
                        done = b.last(NORMS, [("norm", 2)], e)
                        if done is not None:
                            sp.wait_ge(h_ready, done)
                        sp.dma_start(xa[:, :, :], image(x, number + 1)).then_inc(x_loaded, 16)
                    elif e[0] == "save":
                        sp.wait_ge(*taken(b, ("side", 1, "out", T * NQ - 1)))
                        sp.dma_start(image(scratch, number + 1), xa[:, :, :]).then_inc(saved, 16)
                    elif e[0] == "reload":
                        done = b.last(NORMS, [("norm", 3)], e)
                        if done is not None:
                            sp.wait_ge(h_ready, done)
                        sp.wait_ge(saved, b.last(SAVES, [("save",)], e))
                        sp.dma_start(xb[:, :, :], image(scratch, number)).then_inc(reloaded, 16)
                    elif e[0] == "stack":
                        _, layer, m, i = e
                        t, s, part = m // 2, m % 2, slice(i * QW, (i + 1) * QW)
                        low = b.after(PIECES, ("side", layer, "qk", m, i))
                        users = [(2, T * NQ - 1)] if layer == 1 else [(user, NQ * t + NQ - 1) for user in (2, 3)]
                        if layer != 1 and t == T - 1:
                            users.append((1, NQ - 1))
                        used = b.last(SCORES, [("score", user, g, STEPS[user] - 1, 3) for user, g in users], e)
                        if used is not None:
                            sp.wait_ge(score_full, used)
                        sp.wait_ge(lo_ready, low)
                        if layer == 1:
                            q, k = slice(0, HC1), slice(HC1, 2 * HC1)
                            for dst, r, src in ((Q1, 0, hi[i][q]), (Q1, 1, hi[i][q]), (Q1, 2, lo[i][q]),
                                                (K1, 0, hi[i][k]), (K1, 1, lo[i][k]), (K1, 2, hi[i][k])):
                                sp.dma_start(dst[DH * r:DH * (r + 1), part].bitcast(F32),
                                             src.bitcast(F32)).then_inc(stacked[i], 16)
                        else:
                            dst = (Q, K)[s]
                            for r, src in enumerate((hi[i], hi[i], lo[i]) if s == 0 else (hi[i], lo[i], hi[i])):
                                sp.dma_start(dst[DH * r:DH * (r + 1), HPT * t:HPT * (t + 1), part].bitcast(F32),
                                             src[:, :].bitcast(F32)).then_inc(stacked[i], 16)
                    elif e[0] == "maxrow":
                        _, layer, g = e
                        sp.wait_ge(*taken(b, e))
                        if layer == 1:
                            dst = Q1[MAXROW:MAXROW + 2, g * QW:(g + 1) * QW]
                            src = max_rows[MAXROW:MAXROW + 2, :]
                        else:
                            t, qc = g // NQ, g % NQ
                            dst = Q[MAXROW:ROWS, HPT * t:HPT * (t + 1), qc * QW:(qc + 1) * QW]
                            src = max_rows[MAXROW:ROWS, :].unsqueeze(1).broadcast_to([2 * HPT, HPT, QW])
                        sp.dma_start(dst.bitcast(F32), src.bitcast(F32)).then_inc(rows_placed, 16)
                    elif e[0] == "store":
                        sp.wait_ge(*taken(b, ("side", 3, "out", T * NQ - 1)))
                        sp.dma_start(image(out, number - 1), hb[:, :, :]).then_inc(stored, 16)

            run(sp, program, [NORMS, *SIDES, SCORES, PIECES, SAVES])
            sp.wait_ge(stored, STORES.ahead + 16 * B)

        @block.gpsimd
        def _(pool):
            pool.memset(K[MAXROW:ROWS, :, :].bitcast(F32), 0.0).then_inc(kones, 1)
            for j in range(HPT):
                for t in range(T):
                    pool.wait_ge(kones, 1 + 2 * (T * j + t))
                    pool.memset(K[MAXROW:MAXROW + 2 * j + 2, HPT * t + j, :].bitcast(F32), 1.0).then_inc(kones, 1)
                    pool.wait_ge(kones, 2 + 2 * (T * j + t))
                    pool.memset(K[MAXROW:MAXROW + max(2 * j, 1), HPT * t + j, :].bitcast(F32),
                                0.0 if j else 1.0).then_inc(kones, 1)
            pool.wait_ge(set_up, 4)

            def program(b, number):
                for e in b.plan:
                    if e[0] == "power":
                        pool.wait_ge(var_ready, b.after(NORMS, ("norm", e[1])))
                        pool.tensor_tensor(rstd[:, :], gvar[:, :], half_power[:, :], ALU.pow).then_inc(rstd_ready, 1)
                    elif e[0] == "values":
                        _, layer, g, s = e
                        slot, before = prob[VALUES.slot(b, e)], prob[VALUES.slot(b, e) - 1]
                        for add in adds(e):
                            a = add[3]
                            j = a % HPT if layer == 1 else HPT - 1
                            pool.wait_ge(exp_done, b.last(SCORES, [("score", layer, g, s, j)], e))
                            if layer == 1:
                                total, this, first = acc[:, 0, :], slot[:, j, :], slot[:, 0, :]
                            else:
                                total, this, first = acc[:, :, :], slot[:, :, :], before[:, :, :]
                            if a == 1:
                                pool.wait_ge(evacuated, b.until(GROUPS, e))
                            else:
                                pool.wait_ge(added, b.after(ADDS, add, 1))
                            pool.tensor_tensor(total, first if a == 1 else total, this, ALU.add).then_inc(added, 1)

            run(pool, program, [NORMS, SCORES, GROUPS, ADDS])

        @block.scalar
        def _(act):
            act.wait_ge(loaded, 16 * N_LOADS)
            act.activation(ident_bf[:, :], const_sb[:, IDENT:IDENT + P], ACT.Identity).then_inc(set_up, 1)

            def program(b, number):
                for e in b.plan:
                    if e in SIDE.rank[b.n]:
                        bank = bank_of(b.n, e)
                        side_bank, side_full, side_free = side_banks[bank], side_fulls[bank], side_frees[bank]
                    if e[0] == "apply":
                        _, layer, t, i = e
                        first, part = (t, i) == (0, 0), slice(i * QW, (i + 1) * QW)
                        if layer == 3 and first:
                            left = b.last(STORES, [("store",)], e)
                            if left is not None:
                                act.wait_ge(stored, left)
                        if first:
                            act.wait_ge(affine_ready, b.after(NORMS, ("norm", layer)))
                        ins = act.activation(normed[layer][:, t, part], images[layer][:, t, part], ACT.Identity,
                                             bias=gb[:, t:t + 1], scale=ga[:, t:t + 1])
                        if (t, i) == (T - 1, NQ - 1):
                            ins.then_inc(h_ready, 1)
                    elif e[0] == "side":
                        layer, what = e[1], e[2]
                        if layer == 0 and what in ("rows", "turn", "gram", "keys", "attv", "mix"):
                            act.wait_ge(*filled(b, e))
                            if what == "rows":
                                act.copy(su_rows[:, e[3] * C:(e[3] + 1) * C],
                                         side_bank[0:1, 0:C]).then_inc(side_free, 1)
                            elif what == "turn":
                                i = e[3]
                                act.copy(hT[:, 2 * i:2 * i + 2, :].rearrange("p a c -> p (a c)"),
                                         side_bank).then_inc(side_free, 1)
                            else:
                                dst = {"gram": gram, "keys": gk, "attv": attv, "mix": mixT}[what]
                                act.copy(dst[:, :, :].rearrange("p t c -> p (t c)"), side_bank).then_inc(side_free, 1)
                        elif what == "qk":
                            m, i = e[3], e[4]
                            act.wait_ge(stacked[i], b.until(STACKED[i], e))
                            act.wait_ge(*filled(b, e))
                            if layer == 1:
                                act.activation(hi[i][0:2 * HC1, :], side_bank[0:2 * HC1, :],
                                               ACT.Identity).then_inc(hi_ready, 1)
                            else:
                                bias = col(("bq2", "bk2")[m % 2], m // 2) if layer == 2 else const_sb[:, ZERO:ZERO + 1]
                                act.activation(hi[i][:, :], side_bank, ACT.Identity, bias=bias).then_inc(hi_ready, 1)
                        elif what == "v":
                            act.wait_ge(*filled(b, e))
                            i, per = e[3], KC // 2 if layer == 1 else 2
                            act.copy(vT[layer][:, per * i:per * (i + 1), :],
                                     side_bank.rearrange("p (a c) -> p a c", a=per)).then_inc(side_free, 1)
                    elif e[0] == "softmax0":
                        act.wait_ge(l0_ready, b.after(SOFTMAX0, e))
                        act.activation(l0[:, :, :], l0[:, :, :], ACT.Exp, scale=SCALE).then_inc(l0_exp, 1)
                    elif e[0] == "maxrow":
                        if ROWS_PLACED.start[b.n] + ROWS_PLACED.rank[b.n][e] > 16:
                            act.wait_ge(rows_placed, b.after(ROWS_PLACED, e, 16))
                        act.wait_ge(*filled(b, e))
                        n = 2 if e[1] == 1 else 2 * HPT
                        act.copy(max_rows[MAXROW:MAXROW + n, :], side_bank[MAXROW:MAXROW + n, :]).then_inc(side_free, 1)
                    elif e[0] == "evacuate":
                        _, layer, g = e
                        act.wait_ge(*filled(b, ("finish", layer, g)))
                        dst = att1 if layer == 1 else att[:, g // NQ, :]
                        act.copy(dst[:, (g % NQ) * QW:(g % NQ + 1) * QW], values_bank).then_inc(evacuated, 1)
                        before = GROUPS.rank[b.n][("finish", layer, g)] - 1
                        if GROUPS.start[b.n] + before:
                            act.wait_ge(group_done, b.value(GROUPS, before))
                        act.copy(sums[:, :], side_banks[bank_of(b.n, ("finish", layer, g))]).then_inc(
                            side_frees[bank_of(b.n, ("finish", layer, g))], 1)
                    elif e[0] == "score":
                        _, layer, g, s, j = e
                        start = ("score", layer, g, s, 0)
                        if j == 0:
                            lead = STEP_STARTS.start[b.n] - VALUES.start[b.n]
                            used = lead + STEP_STARTS.events[b.n].index(start) + 1 - PROB_SLOTS
                            if VALUES.start[b.n] + used > 0:
                                act.wait_ge(prob_used, b.value(VALUES, used))
                            old = b.steps_back(STEP_STARTS, start, PROB_SLOTS)
                            if old is not None:
                                _, old_layer, old_g, old_s, _ = old
                                a = HPT * old_s + HPT - 1 if old_layer == 1 else max(1, old_s)
                                if old_layer == 1 or old_s < POOLED:
                                    at = ("values", old_layer, old_g, old_s if old_layer == 1 else a)
                                    act.wait_ge(added, b.last(ADDS, [("add", old_layer, old_g, a)], e, at))
                        act.wait_ge(score_full, b.after(SCORES, e))
                        act.activation(prob[STEP_STARTS.slot(b, start)][:, j, :],
                                       score_bank[(SCORES.rank[b.n][e] - 1) % SCORE_BANKS], ACT.Exp,
                                       scale=1.0 if layer == 1 else SCALE).then_inc(exp_done, 1)

            run(act, program, [ROWS_PLACED, GROUPS, NORMS, STORES, *SIDES, *STACKED, SOFTMAX0, SCORES, VALUES, ADDS])

        @block.vector
        def _(dve):
            dve.wait_ge(loaded, 16 * N_LOADS)
            dve.memset(ones[:, :], 1.0).then_inc(set_up, 1)
            dve.memset(half_power[:, :], -0.5).then_inc(set_up, 1)
            dve.memset(count_n[:, :], float(N)).then_inc(set_up, 1)
            dve.wait_ge(biased, 1)
            dve.tensor_tensor(projb2[:, :], side_banks[0][:, 0:T], col("proj2_b"), ALU.add).then_inc(biased, 1)

            def program(b, number):
                for e in b.plan:
                    steps = [0]
                    if e in SIDE.rank[b.n]:
                        bank = bank_of(b.n, e)
                        side_bank, side_full, side_free = side_banks[bank], side_fulls[bank], side_frees[bank]

                    def own(ins):
                        steps[0] += 1
                        ins.then_inc(vstep, 1)
                        dve.wait_ge(vstep, b.after(VSTEPS, e, own_steps(e) - steps[0]))

                    if e[0] == "stats":
                        _, layer, t, i = e
                        if layer == 0 and (t, i) == (0, 0):
                            dve.wait_ge(x_loaded, b.after(LOADS_X, ("load",)))
                        dve.bn_stats(stats[:, t, i, :], images[layer][:, t, i * QW:(i + 1) * QW]).then_inc(vstep, 1)
                        steps[0] += 1
                    elif e[0] == "norm":
                        layer = e[1]
                        dve.wait_ge(vstep, b.after(VSTEPS, ("stats", layer, T - 1, NQ - 1)))
                        dve.sem_inc(turned, 1)
                        for t in range(T):
                            ins = dve.bn_aggr(mv[:, t, :], stats[:, t, :, :].rearrange("p a s -> p (a s)"))
                        own(ins)
                        own(dve.tensor_tensor(small[:, :], mv[:, :, 0], mv[:, :, 0], ALU.mult))
                        dve.tensor_tensor(mv[:, :, 1], mv[:, :, 1], small[:, :], ALU.add).then_inc(moments_ready, 1)
                    elif e[0] == "affine":
                        layer = e[1]
                        dve.wait_ge(rstd_ready, b.after(NORMS, ("norm", layer)))
                        if NORMS.start[b.n] + NORMS.rank[b.n][("norm", layer)] > 1:
                            dve.wait_ge(h_ready, b.after(NORMS, ("norm", layer), 1))
                        own(dve.tensor_tensor(ga[:, :], rstd[:, :], col(f"gn{layer}_scale"), ALU.mult))
                        own(dve.tensor_tensor(small[:, :], gm[:, :, 0], ga[:, :], ALU.mult))
                        own(dve.tensor_tensor(gb[:, :], col(f"gn{layer}_bias"), small[:, :], ALU.subtract))
                        if layer == 0:
                            own(dve.tensor_tensor(small[:, :], mv[:, :, 0], ga[:, :], ALU.mult))
                            own(dve.tensor_tensor(small[:, :], small[:, :], gb[:, :], ALU.add))
                            own(dve.tensor_scalar(hsum[:, :], small[:, :], float(N), None, ALU.mult))
                        dve.sem_inc(affine_ready, 1)
                    elif e[0] == "softmax0":
                        dve.wait_ge(*filled(b, ("side", 0, "logits")))
                        bank = bank_of(b.n, ("side", 0, "logits"))
                        logits = side_banks[bank][:, 0:T * DH].rearrange("p (t d) -> p t d", t=T)
                        own(dve.tensor_reduce(l0max[:, :], logits, AX_X, ALU.max))
                        dve.tensor_tensor(l0[:, :, :], logits, l0max[:, :].unsqueeze(2).broadcast_to([P, T, DH]),
                                          ALU.subtract).then_inc(l0_ready, 1)
                        dve.wait_ge(l0_ready, b.after(SOFTMAX0, e))
                        dve.sem_inc(side_frees[bank], 1)
                        dve.wait_ge(l0_exp, b.after(SOFTMAX0, e))
                        own(dve.tensor_reduce(l0sum[:, :], l0[:, :, :], AX_X, ALU.add))
                        own(dve.reciprocal(l0sum[:, :], l0sum[:, :]))
                        own(dve.tensor_tensor(l0[:, :, :], l0[:, :, :],
                                              l0sum[:, :].unsqueeze(2).broadcast_to([P, T, DH]), ALU.mult))
                        dve.transpose(l0T[:, :, :].rearrange("p t d -> p (t d)"),
                                      l0[:, :, :].rearrange("p t d -> p (t d)")).then_inc(l0T_ready, 1)
                    elif e[0] == "side":
                        layer, what = e[1], e[2]
                        if what == "mean":
                            dve.wait_ge(*filled(b, e))
                            dve.tensor_copy(gm[:, :, :].rearrange("p t s -> p (t s)"),
                                            side_bank[:, 0:2 * T]).then_inc(side_free, 1)
                            dve.wait_ge(*taken(b, e))
                            own(dve.tensor_tensor(small[:, :], gm[:, :, 0], gm[:, :, 0], ALU.mult))
                            dve.scalar_tensor_tensor(gvar[:, :], gm[:, :, 1], EPS, small[:, :], ALU.add,
                                                     ALU.subtract).then_inc(var_ready, 1)
                        elif what == "attb":
                            dve.wait_ge(*filled(b, e))
                            dve.tensor_copy(attb[:, :], side_bank[:, 0:T]).then_inc(side_free, 1)
                        elif what == "projb":
                            dve.wait_ge(*filled(b, e))
                            dve.tensor_tensor(projb0[:, :], side_bank[:, 0:T], col("proj0_b"),
                                              ALU.add).then_inc(side_free, 1)
                        elif what == "qk":
                            dve.wait_ge(hi_ready, b.after(PIECES, e))
                            m, i = e[3], e[4]
                            if layer == 1:
                                dve.tensor_tensor(lo[i][0:2 * HC1, :], side_bank[0:2 * HC1, :],
                                                  hi[i][0:2 * HC1, :].bitcast(F32), ALU.subtract).then_inc(lo_ready, 1)
                            else:
                                bias = col(("bq2", "bk2")[m % 2], m // 2) if layer == 2 else 0.0
                                dve.scalar_tensor_tensor(lo[i][:, :], side_bank, bias, hi[i][:, :].bitcast(F32),
                                                         ALU.add, ALU.subtract).then_inc(lo_ready, 1)
                            dve.wait_ge(lo_ready, b.after(PIECES, e))
                            dve.sem_inc(side_free, 1)
                        elif what == "out":
                            i = e[3]
                            t, part = i // NQ, slice((i % NQ) * QW, (i % NQ + 1) * QW)
                            if layer == 0 and i == 0:
                                dve.wait_ge(*taken(b, ("side", 0, "projb")))
                            if layer == 2 and i == 0:
                                dve.wait_ge(reloaded, b.after(RELOADS, ("reload",)))
                            dve.wait_ge(*filled(b, e))
                            if layer == 0:
                                ins = dve.scalar_tensor_tensor(xa[:, t, part], side_bank, projb0[:, t:t + 1],
                                                               xa[:, t, part], ALU.add, ALU.add)
                            elif layer == 1:
                                ins = dve.scalar_tensor_tensor(xa[:, t, part], side_bank, col("gamma1", 0),
                                                               xa[:, t, part], ALU.mult, ALU.add)
                            elif layer == 2:
                                ins = dve.scalar_tensor_tensor(xb[:, t, part], side_bank, projb2[:, t:t + 1],
                                                               xb[:, t, part], ALU.add, ALU.add)
                            else:
                                ins = dve.scalar_tensor_tensor(hb[:, t, part], side_bank, col("proj3_b", t),
                                                               hb[:, t, part], ALU.add, ALU.add)
                            ins.then_inc(side_free, 1)
                            if i == T * NQ - 1:
                                dve.wait_ge(*taken(b, e))
                    elif e[0] == "max":
                        _, layer, g, a = e
                        dve.wait_ge(max_full, b.after(MAXES, e))
                        bank = max_bank[(MAXES.rank[b.n][e] - 1) % MAX_BANKS]
                        dve.tensor_reduce(maxpart[layer][:, a // NQ, a % NQ:a % NQ + 1], bank, AX_X,
                                          ALU.max).then_inc(max_free, 1)
                    elif e[0] == "split":
                        _, layer, g = e
                        n = MAXIMA[layer] // NQ
                        dve.wait_ge(max_free, b.after(MAXES, ("max", layer, g, MAXIMA[layer] - 1)))
                        own(dve.tensor_reduce(negmax[:, 0:n], maxpart[layer][:, 0:n, :], AX_X, ALU.max, negate=True))
                        if ROWS_PLACED.start[b.n] + ROWS_PLACED.rank[b.n][("maxrow", layer, g)] > 16:
                            dve.wait_ge(rows_placed, b.after(ROWS_PLACED, ("maxrow", layer, g), 16))
                        own(dve.tensor_copy(maxsplit[:, 0:n, 0], negmax[:, 0:n]))
                        dve.tensor_tensor(maxsplit[:, 0:n, 1], negmax[:, 0:n], maxsplit[:, 0:n, 0],
                                          ALU.subtract).then_inc(maxsplit_ready, 1)
                    elif e[0] == "divide":
                        _, layer, g, i = e
                        part = slice(i * P, (i + 1) * P)
                        dst = (att1 if layer == 1 else att[:, g // NQ, :])[:, (g % NQ) * QW:(g % NQ + 1) * QW]
                        if i == 0:
                            dve.wait_ge(evacuated, b.last(GROUPS, [("finish", layer, g)], e))
                            dve.wait_ge(*taken(b, ("finish", layer, g)))
                        own(dve.reciprocal(sums[:, part], sums[:, part]))
                        ins = dve.tensor_tensor(dst[:, part], dst[:, part], sums[:, part], ALU.mult)
                        if i == QT - 1:
                            ins.then_inc(group_done, 1)
                    assert steps[0] == own_steps(e), (e, steps)

            run(dve, program, [ROWS_PLACED, LOADS_X, VSTEPS, NORMS, *SIDES, SOFTMAX0, PIECES, RELOADS, MAXES, GROUPS])

        @block.tensor
        def _(pe):
            pe.wait_ge(loaded, 16 * N_LOADS)
            pe.wait_ge(set_up, 4)
            pe.wait_ge(kones, 1 + 2 * HEADS)
            for ot in range(T):
                for t in range(T):
                    ins = pe.matmul(side_banks[0][:, ot:ot + 1], wp_sb[2][:, t, ot * P:(ot + 1) * P], col("bv2", t),
                                    start=(t == 0), stop=(t == T - 1))
            ins.then_inc(biased, 1)
            pe.wait_ge(biased, 2)
            ident = const_sb[:, IDENT:IDENT + P]

            def program(b, number):
                for e in b.plan:
                    if e[0] == "begin":
                        chunk, piece = e[1], ("side",) + e[2:]
                    else:
                        chunk, piece = chunks(e) - 1, e
                    if e[0] == "values" and e[1] != 1 and e[3] == KC - 1 and POOLED < KC:
                        piece = ("finish",) + e[1:3]
                    if piece in SIDE.rank[b.n]:
                        bank = bank_of(b.n, piece)
                        side_bank, side_full = side_banks[bank], side_fulls[bank]
                    if piece in SIDE.rank[b.n] and chunk == 0 and (e[0] != "finish" or e[1] == 1 or POOLED == KC):
                        pe.wait_ge(side_frees[bank], b.after(SIDES[bank], piece, 1))
                    if piece in NEEDS and chunk == 0:
                        pe.wait_ge(*taken(b, NEEDS[piece]))
                    if piece[0] == "side":
                        layer, what = piece[1], piece[2]

                        def share(parts):
                            parts = list(parts)
                            n = chunks(piece)
                            return parts[chunk * len(parts) // n:(chunk + 1) * len(parts) // n]

                        if what == "mean":
                            pe.wait_ge(moments_ready, b.after(NORMS, ("norm", layer)))
                            mean = MEAN8 if layer == 0 else MEAN32
                            ins = pe.matmul(side_bank[:, 0:2 * T], const_sb[:, mean:mean + P],
                                            mv[:, :, :].rearrange("p t s -> p (t s)"), start=True, stop=True)
                        elif what == "rows":
                            pe.wait_ge(h_ready, b.after(NORMS, ("norm", 0)))
                            if e[3] == 0:
                                for t in range(T):
                                    ins = pe.matmul(side_bank[0:1, t * P:(t + 1) * P], hsum[:, t:t + 1], ident,
                                                    start=True, stop=True)
                            else:
                                for t in range(T):
                                    pe.matmul(side_bank[0:1, 0:C], hsum[:, t:t + 1], wqk0_sb[:, t, C:2 * C],
                                              start=(t == 0), stop=False)
                                ins = pe.matmul(side_bank[0:1, 0:C], count_n[:, :], rows0_sb[:, C:2 * C],
                                                start=False, stop=True)
                        elif what == "turn":
                            for a in range(2):
                                for t in range(T):
                                    kt = 2 * piece[3] + a
                                    ins = pe.transpose(side_bank[:, a * C + t * P:a * C + (t + 1) * P],
                                                       ha[:, t, kt * P:(kt + 1) * P], ident)
                        elif what == "gram":
                            for t, kt in share((t, kt) for t in range(T) for kt in range(KC)):
                                ins = pe.matmul(side_bank[:, t * C:(t + 1) * C], hT[:, kt, t * P:(t + 1) * P],
                                                hT[:, kt, :], start=(kt == 0), stop=(kt == KC - 1))
                        elif what == "keys":
                            for it in share(range(T)):
                                dst = side_bank[:, it * C:(it + 1) * C]
                                for t in range(T):
                                    pe.matmul(dst, gram[:, t, it * P:(it + 1) * P], wqk0_sb[:, t, C:2 * C],
                                              start=(t == 0), stop=False)
                                ins = pe.matmul(dst, su_rows[:, it * P:(it + 1) * P], rows0_sb[:, C:2 * C],
                                                start=False, stop=True)
                        elif what == "logits":
                            for t in range(T):
                                for j in range(HPT):
                                    ch = slice((HPT * t + j) * DH, (HPT * t + j + 1) * DH)
                                    dst = side_bank[head_rows(j), t * DH:(t + 1) * DH]
                                    for k in range(T):
                                        pe.matmul(dst, wqk0_sb[:, k, ch], gk[:, k, ch], start=(k == 0), stop=False,
                                                  tile_position=(0, DH * j))
                                    ins = pe.matmul(dst, rows0_sb[:, ch], su_rows[:, C + ch.start:C + ch.stop],
                                                    start=False, stop=True, tile_position=(0, DH * j))
                        elif what == "attv":
                            pe.wait_ge(l0T_ready, b.after(SOFTMAX0, ("softmax0",)))
                            pe.sem_inc(turned, 1)
                            for t in range(T):
                                for j in range(HPT):
                                    r = head_rows(j)
                                    ins = pe.matmul(side_bank[r, t * C:(t + 1) * C], l0T[r, t, :], wv0_sb[r, t, :],
                                                    start=True, stop=True, tile_position=(DH * j, DH * j))
                        elif what == "attb":
                            pe.sem_inc(turned, 1)
                            for t in range(T):
                                for j in range(HPT):
                                    r = head_rows(j)
                                    ins = pe.matmul(side_bank[r, t:t + 1], l0T[r, t, :], col("bv0", t)[r, :],
                                                    start=True, stop=True, tile_position=(DH * j, DH * j))
                        elif what == "projb":
                            for ot in range(T):
                                for t in range(T):
                                    ins = pe.matmul(side_bank[:, ot:ot + 1], wp_sb[0][:, t, ot * P:(ot + 1) * P],
                                                    attb[:, t:t + 1], start=(t == 0), stop=(t == T - 1))
                        elif what == "mix":
                            for it in share(range(T)):
                                for t in range(T):
                                    ins = pe.matmul(side_bank[:, it * C:(it + 1) * C],
                                                    attv[:, t, it * P:(it + 1) * P], wp_sb[0][:, t, :],
                                                    start=(t == 0), stop=(t == T - 1))
                        elif what == "qk":
                            m, i = piece[3], piece[4]
                            part = slice(i * QW, (i + 1) * QW)
                            if layer == 1:
                                for t in share(range(T)):
                                    ins = pe.matmul(side_bank[0:2 * HC1, :], wa1_sb[:, t, 0:2 * HC1], xa[:, t, part],
                                                    start=(t == 0), stop=(t == T - 1))
                            else:
                                if m == 0 and i == 0 and chunk == 0:
                                    pe.wait_ge(h_ready, b.after(NORMS, ("norm", layer)))
                                o = (m % 2) * C + (m // 2) * P
                                for t in share(range(T)):
                                    ins = pe.matmul(side_bank, wqkv_sb[layer][:, t, o:o + P],
                                                    normed[layer][:, t, part], start=(t == 0), stop=(t == T - 1))
                        elif what == "v":
                            per, width = (KC // 2, VC1) if layer == 1 else (2, C)
                            src, w, o = (xa, wa1_sb, 2 * HC1) if layer == 1 else (normed[layer], wqkv_sb[layer], 2 * C)
                            for a in share(range(per)):
                                kt = per * piece[3] + a
                                for t in range(T):
                                    ins = pe.matmul(side_bank[:, a * width:(a + 1) * width],
                                                    src[:, t, kt * P:(kt + 1) * P], w[:, t, o:o + width],
                                                    start=(t == 0), stop=(t == T - 1))
                        elif what == "out":
                            i = piece[3]
                            ot, part = i // NQ, slice((i % NQ) * QW, (i % NQ + 1) * QW)
                            if layer != 0 and i == 0 and chunk == 0:
                                g = NQ - 1 if layer == 1 else T * NQ - 1
                                pe.wait_ge(group_done, b.last(GROUPS, [("finish", layer, g)], e))
                            if layer == 1:
                                ins = pe.matmul(side_bank, wo1_sb[:, ot * P:(ot + 1) * P], att1[:, part],
                                                start=True, stop=True)
                            else:
                                w, src = (mixT, ha) if layer == 0 else (wp_sb[layer], att)
                                for t in share(range(T)):
                                    ins = pe.matmul(side_bank, w[:, t, ot * P:(ot + 1) * P], src[:, t, part],
                                                    start=(t == 0), stop=(t == T - 1))
                        if e[0] == "side":
                            ins.then_inc(side_full, 1)
                    elif e[0] == "max":
                        _, layer, g, a = e
                        r = MAXES.rank[b.n][e]
                        if MAXES.start[b.n] + r > MAX_BANKS:
                            pe.wait_ge(max_free, b.after(MAXES, e, MAX_BANKS))
                        half = slice((a % NQ) * QW, (a % NQ + 1) * QW)
                        if a == 0 and (layer == 1 and g == 0 or layer != 1 and g % NQ == 0):
                            ms = [0] if layer == 1 else [g // NQ * 2, g // NQ * 2 + 1]
                            for i in range(2):
                                pe.wait_ge(stacked[i], b.last(STACKED[i], [("stack", layer, m, i) for m in ms], e))
                        if layer == 1:
                            q = (g * QT + a // NQ) * P
                            left, right = Q1[0:SPLIT, q:q + P], K1[0:SPLIT, half]
                        else:
                            t, qc = g // NQ, g % NQ
                            qt, j = a // NQ // HPT, a // NQ % HPT
                            q = (qc * QT + qt) * P
                            left, right = Q[0:SPLIT, HPT * t + j, q:q + P], K[0:SPLIT, HPT * t + j, half]
                        pe.matmul(max_bank[(r - 1) % MAX_BANKS], left, right,
                                  start=True, stop=True).then_inc(max_full, 1)
                    elif e[0] == "maxrow":
                        _, layer, g = e
                        pe.wait_ge(maxsplit_ready, b.after(SPLITS, ("split", layer, g)))
                        w = 1 if layer == 1 else HPT
                        for qt in range(QT):
                            ins = pe.matmul(side_bank[MAXROW:MAXROW + 2 * w, qt * P:(qt + 1) * P],
                                            maxsplit[:, qt * w:(qt + 1) * w, :].rearrange("p j s -> p (j s)"),
                                            ident_bf[:, :], start=True, stop=True, tile_position=(0, MAXROW))
                        ins.then_inc(side_full, 1)
                    elif e[0] == "score":
                        _, layer, g, s, j = e
                        r = SCORES.rank[b.n][e]
                        if r > SCORE_BANKS:
                            pe.wait_ge(exp_done, b.after(SCORES, e, SCORE_BANKS))
                        elif SCORES.start[b.n]:
                            pe.wait_ge(exp_done, b.before(SCORES))
                        if s == 0 and j == 0:
                            pe.wait_ge(rows_placed, b.last(ROWS_PLACED, [("maxrow", layer, g)], e))
                        if layer == 1:
                            kt = HPT * s + j
                            left, right = K1[0:MAXROW + 2, kt * P:(kt + 1) * P], Q1[0:MAXROW + 2, g * QW:(g + 1) * QW]
                        else:
                            t, qc = g // NQ, g % NQ
                            left = K[0:ROWS, HPT * t + j, s * P:(s + 1) * P]
                            right = Q[0:ROWS, HPT * t + j, qc * QW:(qc + 1) * QW]
                        pe.matmul(score_bank[(r - 1) % SCORE_BANKS], left, right,
                                  start=True, stop=True).then_inc(score_full, 1)
                    elif e[0] in ("value", "values"):
                        layer, g, s = e[1:4]
                        j = e[4] if e[0] == "value" else HPT - 1
                        slot = prob[VALUES.slot(b, ("values", layer, g, s))]
                        if s == 0 and j == 0 and GROUPS.start[b.n] + GROUPS.events_before(b, e):
                            pe.wait_ge(evacuated, b.until(GROUPS, e))
                        if s == 0 and j == 0:
                            values = ("side", layer, "v", 1 if layer == 1 else KC // 2 - 1)
                            if values in SIDE.rank[b.n] and b.place[values] < b.place[e]:
                                pe.wait_ge(*taken(b, values))
                        pe.wait_ge(exp_done, b.last(SCORES, [("score", layer, g, s, j)], e))
                        if layer == 1:
                            kt = HPT * s + j
                            ins = pe.matmul(values_bank, vT1[:, kt, :], slot[:, j, :],
                                            start=(kt == 0), stop=(kt == KC - 1))
                        else:
                            head = HPT * (g // NQ) + j
                            ins = pe.matmul(values_bank[head_rows(j), :], vT[layer][:, s, head * DH:(head + 1) * DH],
                                            slot[:, j, :], start=(s == 0), stop=(s == KC - 1),
                                            tile_position=(0, DH * j))
                        if e[0] == "values":
                            if layer != 1 and s == KC - 1 and POOLED < KC:
                                for own in range(POOLED, KC):
                                    tiles = prob[VALUES.slot(b, ("values", layer, g, own))]
                                    for j in range(HPT):
                                        ins = pe.matmul(side_bank[head_rows(j), :], ones[:, :], tiles[:, j, :],
                                                        start=(own == POOLED), stop=False, tile_position=(0, DH * j))
                                ins.then_inc(prob_used, KC - POOLED)
                            elif layer == 1 or s < POOLED:
                                ins.then_inc(prob_used, 1)
                    elif e[0] == "finish":
                        _, layer, g = e
                        add = ("add", layer, g, (KC if layer == 1 else POOLED) - 1)
                        at = ("values", layer, g, STEPS[1] - 1 if layer == 1 else POOLED - 1)
                        pe.wait_ge(added, b.last(ADDS, [add], e, at))
                        for j in range(HPT):
                            ins = pe.matmul(side_bank[head_rows(j), :], ones[:, :], acc[:, 0 if layer == 1 else j, :],
                                            start=(layer == 1 or POOLED == KC), stop=True, tile_position=(0, DH * j))
                        ins.then_inc(side_full, 1)

            run(pe, program, [ROWS_PLACED, *SIDES, NORMS, SOFTMAX0, GROUPS, MAXES, *STACKED, SPLITS, SCORES, ADDS])


def kernel(**inputs):
    import numpy as np
    import concourse.bacc as bacc
    from concourse.bass_utils import run_bass_kernel_spmd

    a = {k: np.asarray(v) for k, v in inputs.items()}

    def column(v):
        return v.reshape(T, P).T

    def beside(v):
        return v.reshape(T, HPT, DH, -1).transpose(0, 2, 1, 3).reshape(v.shape)

    def qkv(w):
        return np.concatenate([beside(w[:C]), beside(w[C:2 * C]), w[2 * C:]]).T

    cols = [a["L0_conv_gn_scale"], a["L0_conv_gn_bias"], a["L0_conv_qkv_b"][2 * C:], a["L0_conv_proj_b"],
            a["L2_conv_gn_weight"], a["L2_conv_gn_bias"], beside(a["L2_conv_qkv_bias"][:C]),
            beside(a["L2_conv_qkv_bias"][C:2 * C]), a["L2_conv_qkv_bias"][2 * C:], a["L2_conv_proj_bias"],
            a["L3_conv_gamma"], a["L3_conv_beta"], a["L3_conv_b_out"], np.broadcast_to(a["L1_conv_gamma"], (C,))]
    consts = np.zeros((P, CONST_COLS), np.float32)
    for i in range(P):
        consts[i, IDENT + i] = 1.0
        for at, width in ((MEAN8, C // 32), (MEAN32, C // 8)):
            consts[i, at + i // width * width:at + (i // width + 1) * width] = 1.0 / width
    arrays = {
        "x": a["x"].reshape(B, C, N),
        "wqk0T": a["L0_conv_qkv_w"][:2 * C].T, "wv0": a["L0_conv_qkv_w"][2 * C:], "wp0T": a["L0_conv_proj_w"].T,
        "rows0": a["L0_conv_qkv_b"][:2 * C].reshape(1, 2 * C),
        "waT1": a["L1_conv_Wa"].T, "woT1": a["L1_conv_Wo"].T,
        "wqkv2T": qkv(a["L2_conv_qkv_weight"]), "wp2T": a["L2_conv_proj_weight"].T,
        "wqkv3T": qkv(a["L3_conv_w_qkv"]), "wp3T": a["L3_conv_w_out"].T,
        "cols": np.concatenate([column(v) for v in cols], axis=1), "consts": consts,
    }
    arrays = {k: np.ascontiguousarray(v) for k, v in arrays.items()}
    nc = bacc.Bacc("TRN2", target_bir_lowering=False, num_devices=1)
    args = {k: nc.dram_tensor(f"in_{k}", v.shape, F32, kind="ExternalInput").ap() for k, v in arrays.items()}
    scratch = nc.dram_tensor("scratch", (B, C, N), F32, kind="Internal").ap()
    out = nc.dram_tensor("out_0", (B, C, N), F32, kind="ExternalOutput").ap()
    build(nc, **args, scratch=scratch, out=out)
    r = run_bass_kernel_spmd(nc, [{f"in_{k}": v for k, v in arrays.items()}], core_ids=[0])
    return r.results[0]["out_0"].reshape(B, C, 32, 32)
```
